# Optimizing a Trainium2 kernel written in Bass

```python
import numpy as np
import jax
import jax.numpy as jnp

def _softmax(x, axis=-1):
    return jax.nn.softmax(x, axis=axis)

def _gelu(x):
    return jax.nn.gelu(x, approximate=True)

def _silu(x):
    return jax.nn.silu(x)

def _sigmoid(x):
    return jax.nn.sigmoid(x)

def _layernorm(x, axis=-1, eps=1e-05):
    m = jnp.mean(x, axis=axis, keepdims=True)
    v = jnp.var(x, axis=axis, keepdims=True)
    return (x - m) / jnp.sqrt(v + eps)

def _scatter_add(tgt, idx, src, axis=0):
    return tgt.at[idx].add(src)

def _segment_sum(src, seg, n):
    return jax.ops.segment_sum(src, seg, n)
kernel_name = 'mk_adj_resnorm_d4_adj_r2_a0c6b2'

def setup_inputs(seed: int=0):
    np.random.seed(seed)
    _w = jnp.asarray

    def _rec_inputs():
        import jax
        import jax.numpy as jnp
        _gk = jax.random.key(seed)
        x = -6.503e-05 + 0.07158 * jax.random.normal(jax.random.fold_in(_gk, 1), (4096, 128), jnp.float32)
        _w = (1.0 + jnp.arange(4096, dtype=jnp.float32)) ** (-0.5)
        _w = _w / _w.mean()
        _pij = jnp.clip(0.00195312 * _w[:, None] * _w[None, :], 0.0, 1.0)
        _a = jax.random.uniform(jax.random.fold_in(_gk, 2), (4096, 4096)) < _pij
        _a = jnp.logical_or(_a, jnp.eye(4096, dtype=bool))
        _af = _a.astype(jnp.float32)
        _af = _af / jnp.maximum(_af.sum(-1, keepdims=True), 1.0)
        adj = _af
        return (x, adj)
    x, adj = _rec_inputs()

    def _L0_gnn_setup():
        import jax, jax.numpy as jnp
        import numpy as np
        EPS = 1e-05
        MIN_NORM = 1e-15

        def _norm(x):
            return jnp.maximum(jnp.linalg.norm(x, axis=-1, keepdims=True), MIN_NORM)

        def _artanh(x):
            return jnp.arctanh(jnp.clip(x, -1.0 + EPS, 1.0 - EPS))

        def expmap0(u):
            un = _norm(u)
            return jnp.tanh(un) * u / un

        def logmap0(y):
            yn = _norm(y)
            return _artanh(yn) * y / yn

        def mobius_matvec(W, x):
            mx = x @ W
            xn = _norm(x)
            mxn = _norm(mx)
            res = jnp.tanh(mxn / xn * _artanh(xn)) * mx / mxn
            zero = jnp.all(mx == 0.0, axis=-1, keepdims=True)
            return jnp.where(zero, 0.0, res)

        def mobius_scalar_mul(r, x):
            xn = _norm(x)
            return jnp.tanh(r * _artanh(xn)) * x / xn

        def _clamp_abs(x, eps=1e-10):
            return jnp.where(x >= 0.0, jnp.maximum(x, eps), jnp.minimum(x, -eps))
        key = jax.random.key(seed)
        k1, k2, k3 = jax.random.split(key, 3)
        N, D_IN, D_OUT = (4096, 128, 128)
        AVG_DEG = 64.0
        v = 0.1 * jax.random.normal(k1, (N, D_IN), dtype=jnp.float32)
        X = expmap0(v)
        mask = (jax.random.uniform(k2, (N, N)) < AVG_DEG / N).astype(jnp.float32)
        mask = mask + jnp.eye(N, dtype=jnp.float32)
        A_hat = mask / mask.sum(-1, keepdims=True)
        W = jax.random.uniform(k3, (D_IN, D_OUT), dtype=jnp.float32)
        return {'X': X, 'A_hat': A_hat, 'W': W}
    _L0_gnn_all = _L0_gnn_setup()
    _L0_gnn_in = {k: v for k, v in _L0_gnn_all.items() if k in ('W',)}
    del _L0_gnn_all

    def _L1_gnn_setup():
        import jax, jax.numpy as jnp
        import numpy as np
        N = 4096
        IN_C = 128
        OUT_C = 128
        key = jax.random.key(seed)
        k_x, k_adj, k_w, k_b = jax.random.split(key, 4)
        x = jax.random.normal(k_x, (N, IN_C), dtype=jnp.float32)
        adj = jax.random.uniform(k_adj, (N, N), dtype=jnp.float32)
        bound = 1.0 / np.sqrt(IN_C)
        W = jax.random.uniform(k_w, (OUT_C, IN_C), dtype=jnp.float32, minval=-bound, maxval=bound)
        b = jax.random.uniform(k_b, (OUT_C,), dtype=jnp.float32, minval=-bound, maxval=bound)
        return {'x': x, 'adj': adj, 'W': W, 'b': b}
    _L1_gnn_all = _L1_gnn_setup()
    _L1_gnn_in = {k: v for k, v in _L1_gnn_all.items() if k in ('W', 'b')}
    del _L1_gnn_all

    def _L2_gnn_setup():
        import jax, jax.numpy as jnp
        import numpy as np
        N, D = (4096, 128)
        EDGE_PROB = 0.005
        COS_EPS = 1e-08
        key = jax.random.key(seed)
        kx, ka = jax.random.split(key)
        x = jax.random.normal(kx, (N, D), dtype=jnp.float32)
        adj = (jax.random.uniform(ka, (N, N)) < EDGE_PROB).astype(jnp.float32)
        return {'t': jnp.float32(0.0), 'x': x, 'adj': adj, 'alpha': jnp.float32(0.5), 'beta': jnp.float32(1.0)}
    _L2_gnn_all = _L2_gnn_setup()
    _L2_gnn_in = {k: v for k, v in _L2_gnn_all.items() if k in ('t', 'alpha', 'beta')}
    del _L2_gnn_all

    def _L3_gnn_setup():
        import jax, jax.numpy as jnp
        import numpy as np
        N, DIM = (8192, 128)

        def _gru_cell(x, h, W_ih, W_hh, b_ih, b_hh):
            gi = x @ W_ih.T + b_ih
            gh = h @ W_hh.T + b_hh
            i_r, i_z, i_n = jnp.split(gi, 3, axis=-1)
            h_r, h_z, h_n = jnp.split(gh, 3, axis=-1)
            r = jax.nn.sigmoid(i_r + h_r)
            z = jax.nn.sigmoid(i_z + h_z)
            n = jnp.tanh(i_n + r * h_n)
            return (1.0 - z) * n + z * h
        key = jax.random.key(seed)
        ks = jax.random.split(key, 8)
        states = jax.random.normal(ks[0], (N, DIM), dtype=jnp.float32)
        adj = jax.random.uniform(ks[1], (N, N), dtype=jnp.float32)
        s = 1.0 / np.sqrt(DIM)
        W_msg = jax.random.uniform(ks[2], (DIM, DIM), minval=-s, maxval=s, dtype=jnp.float32)
        b_msg = jax.random.uniform(ks[3], (DIM,), minval=-s, maxval=s, dtype=jnp.float32)
        W_ih = jax.random.uniform(ks[4], (3 * DIM, DIM), minval=-s, maxval=s, dtype=jnp.float32)
        W_hh = jax.random.uniform(ks[5], (3 * DIM, DIM), minval=-s, maxval=s, dtype=jnp.float32)
        b_ih = jax.random.uniform(ks[6], (3 * DIM,), minval=-s, maxval=s, dtype=jnp.float32)
        b_hh = jax.random.uniform(ks[7], (3 * DIM,), minval=-s, maxval=s, dtype=jnp.float32)
        return {'states': states, 'adj': adj, 'W_msg': W_msg, 'b_msg': b_msg, 'W_ih': W_ih, 'W_hh': W_hh, 'b_ih': b_ih, 'b_hh': b_hh}
    _L3_gnn_all = _L3_gnn_setup()
    _L3_gnn_in = {k: v for k, v in _L3_gnn_all.items() if k in ('W_msg', 'b_msg', 'W_ih', 'W_hh', 'b_ih', 'b_hh')}
    del _L3_gnn_all
    return {'x': x, 'adj': adj, 'L0_gnn_W': _L0_gnn_in['W'], 'L1_gnn_W': _L1_gnn_in['W'], 'L1_gnn_b': _L1_gnn_in['b'], 'L2_gnn_t': _L2_gnn_in['t'], 'L2_gnn_alpha': _L2_gnn_in['alpha'], 'L2_gnn_beta': _L2_gnn_in['beta'], 'L3_gnn_W_msg': _L3_gnn_in['W_msg'], 'L3_gnn_b_msg': _L3_gnn_in['b_msg'], 'L3_gnn_W_ih': _L3_gnn_in['W_ih'], 'L3_gnn_W_hh': _L3_gnn_in['W_hh'], 'L3_gnn_b_ih': _L3_gnn_in['b_ih'], 'L3_gnn_b_hh': _L3_gnn_in['b_hh']}

def reference(x, adj, L0_gnn_W, L1_gnn_W, L1_gnn_b, L2_gnn_t, L2_gnn_alpha, L2_gnn_beta, L3_gnn_W_msg, L3_gnn_b_msg, L3_gnn_W_ih, L3_gnn_W_hh, L3_gnn_b_ih, L3_gnn_b_hh):
    import jax
    import jax.numpy as jnp

    def _L0_gnn_ref(X, A_hat, W):
        import jax, jax.numpy as jnp
        import numpy as np
        EPS = 1e-05
        MIN_NORM = 1e-15

        def _norm(x):
            return jnp.maximum(jnp.linalg.norm(x, axis=-1, keepdims=True), MIN_NORM)

        def _artanh(x):
            return jnp.arctanh(jnp.clip(x, -1.0 + EPS, 1.0 - EPS))

        def expmap0(u):
            un = _norm(u)
            return jnp.tanh(un) * u / un

        def logmap0(y):
            yn = _norm(y)
            return _artanh(yn) * y / yn

        def mobius_matvec(W, x):
            mx = x @ W
            xn = _norm(x)
            mxn = _norm(mx)
            res = jnp.tanh(mxn / xn * _artanh(xn)) * mx / mxn
            zero = jnp.all(mx == 0.0, axis=-1, keepdims=True)
            return jnp.where(zero, 0.0, res)

        def mobius_scalar_mul(r, x):
            xn = _norm(x)
            return jnp.tanh(r * _artanh(xn)) * x / xn

        def _clamp_abs(x, eps=1e-10):
            return jnp.where(x >= 0.0, jnp.maximum(x, eps), jnp.minimum(x, -eps))
        XW = mobius_matvec(W, X)
        sq = jnp.sum(XW * XW, axis=-1, keepdims=True)
        gamma = 2.0 / jnp.maximum(1.0 - sq, EPS)
        nominator = A_hat @ (gamma * XW)
        denominator = _clamp_abs(A_hat @ (gamma - 1.0))
        two_mean = nominator / denominator
        m = mobius_scalar_mul(0.5, two_mean)
        r = A_hat.sum(-1, keepdims=True)
        AXW = mobius_scalar_mul(r, m)
        return expmap0(jax.nn.relu(logmap0(AXW)))

    def _L1_gnn_ref(x, adj, W, b):
        import jax, jax.numpy as jnp
        import numpy as np
        N = 4096
        IN_C = 128
        OUT_C = 128
        n = adj.shape[0]
        a_hat = adj + jnp.eye(n, dtype=adj.dtype)
        deg = jnp.sum(a_hat, axis=1)
        d_inv_sqrt = jnp.power(deg, -0.5)
        d_inv_sqrt = jnp.where(jnp.isinf(d_inv_sqrt), 0.0, d_inv_sqrt)
        norm_adj = a_hat * d_inv_sqrt[:, None] * d_inv_sqrt[None, :]
        support = norm_adj @ x
        return support @ W.T + b

    def _L2_gnn_ref(t, x, adj, alpha, beta):
        import jax, jax.numpy as jnp
        import numpy as np
        N, D = (4096, 128)
        EDGE_PROB = 0.005
        COS_EPS = 1e-08
        deg = jnp.clip(adj.sum(axis=1), 1.0)
        dis = deg ** (-0.5)
        adj_norm = dis[:, None] * adj * dis[None, :]
        diffusion = adj_norm @ x - x
        norms = jnp.maximum(jnp.linalg.norm(x, axis=-1), COS_EPS)
        sim = x @ x.T / (norms[:, None] * norms[None, :])
        attn = jax.nn.softmax(beta * sim * adj, axis=1)
        attn = jax.lax.stop_gradient(attn)
        return diffusion + jax.nn.sigmoid(alpha) * (attn @ x - x)

    def _L3_gnn_ref(states, adj, W_msg, b_msg, W_ih, W_hh, b_ih, b_hh):
        import jax, jax.numpy as jnp
        import numpy as np
        N, DIM = (8192, 128)

        def _gru_cell(x, h, W_ih, W_hh, b_ih, b_hh):
            gi = x @ W_ih.T + b_ih
            gh = h @ W_hh.T + b_hh
            i_r, i_z, i_n = jnp.split(gi, 3, axis=-1)
            h_r, h_z, h_n = jnp.split(gh, 3, axis=-1)
            r = jax.nn.sigmoid(i_r + h_r)
            z = jax.nn.sigmoid(i_z + h_z)
            n = jnp.tanh(i_n + r * h_n)
            return (1.0 - z) * n + z * h
        agg = adj @ states
        msg = jax.nn.relu(agg @ W_msg.T + b_msg)
        return _gru_cell(msg, states, W_ih, W_hh, b_ih, b_hh)
    x = _layernorm(x + _L0_gnn_ref(x, adj, L0_gnn_W), axis=-1)
    x = _layernorm(x + _L1_gnn_ref(x, adj, L1_gnn_W, L1_gnn_b), axis=-1)
    x = _layernorm(x + _L2_gnn_ref(L2_gnn_t, x, adj, L2_gnn_alpha, L2_gnn_beta), axis=-1)
    x = _layernorm(x + _L3_gnn_ref(x, adj, L3_gnn_W_msg, L3_gnn_b_msg, L3_gnn_W_ih, L3_gnn_W_hh, L3_gnn_b_ih, L3_gnn_b_hh), axis=-1)
    return x

_drawn_inputs = setup_inputs


def setup_inputs(seed=0):
    import zlib

    import numpy as np

    out = dict(_drawn_inputs(seed))
    spreads = {}
    factors = {'L3_gnn_b_msg': 8.0, 'L3_gnn_b_ih': 3.073, 'L3_gnn_b_hh': 4.967}
    for name, (base, spread) in spreads.items():
        noise = np.random.default_rng([zlib.crc32(name.encode()), seed]).standard_normal(out[name].shape)
        drawn = base * np.exp(spread * noise) if base else spread * noise
        out[name] = jnp.asarray(drawn.astype(out[name].dtype))
    for name, factor in factors.items():
        out[name] = (out[name] * factor).astype(out[name].dtype)
    return out
```

```python
from contextlib import ExitStack

import concourse.bass as bass
import numpy as np
from concourse import mybir

F32 = mybir.dt.float32
F32R = mybir.dt.float32r
F16 = mybir.dt.float16
ALU = mybir.AluOpType
ACT = mybir.ActivationFunctionType
AX = mybir.AxisListType

P = 128
N = 4096
D = 128
NB = N // P
Q = 4
SLAB = Q * P
SLABS = N // SLAB
BANKS = 4
AHEAD = 3
YW = 2 * D + 4
LO = D + 2

EPS = 1e-5
MIN_NORM = 1e-15
DEN_EPS = 1e-10
COS_EPS = 1e-8
TINY_ARTANH = 0.125
ARTANH_MAX = float(np.arctanh(np.float32(1.0 - EPS)))
XN_SCALE = 16.0
NEG_HUGE = -3.0e38
LOADS = 16

PLAIN = [("A", j) for j in range(NB)]
ATTEND = [("A", 0), ("A", 1)]
for _g in range(8):
    for _i in range(4):
        ATTEND.append(("S", 4 * _g + _i))
        if _i < 3:
            ATTEND.append(("A", 2 + 3 * _g + _i))
ATTEND += [("A", j) for j in range(26, NB)] + [("B", j) for j in range(NB)]
FILLS = [PLAIN, PLAIN, ATTEND, PLAIN]

LN = ["ln_stats", "ln_aggr", "ln_eps", "ln_rstd", "ln_bias", "ln_out"]
ARTANH = ["one_minus", "inv_minus", "ratio", "log", "z", "h1", "h2", "h3", "h4", "series", "differ", "choose", "artanh"]
ROWS = [
    ["sum_parts", "sum_den", "square", "sum_square", "den_up", "den_down", "den_gap", "den_side", "den",
     "inv_den", "inv_den2", "norm2", "norm", "norm_floor", "inv_norm", "clip"] + ARTANH
    + ["scale", "scale_clip", "scale_row", "scale_unit", "times_scale", "relu", "square_u", "sum_u", "clamp_u",
       "norm_u", "inv_u", "tanh_u", "scale_u", "times_u", "add_x",
       "row_sum", "deg", "deg_zero", "deg_safe", "deg_pow", "deg_keep", "dcol", "dis_clip", "dis"] + LN,
    ["times_w", "x_bias", "d_copy", "combine"] + LN
    + ["square_x", "sum_x", "clamp_x", "unit_scale", "unit", "turn_unit", "unit_high", "unit_low"],
    ["turn_back", "sum_exp", "inv_sum", "att_scale", "dis_rows", "x_sum", "x_scale", "combine_diff",
     "combine_att"] + LN,
    ["message", "message_act", "stage", "turn_h", "h_copy", "gate_r", "r_act", "gate_z", "z_act",
     "hidden_n", "r_half", "r_times", "input_n", "n_in", "n_act", "z_half", "h_minus_n", "z_times", "h_new",
     "turn_new", "combine"] + LN,
]
(DEN, SS, UP, DOWN, GAP, SIDE, INV, NRM, INV_NRM, CLIP, MINUS, RATIO, LOG, Z, H, SER, ART, SCL, RS, DEG, ZERO,
 SAFE, VAR, RSTD, BIAS) = range(25)
(X_SS, M_SS, X_N, M_N, G_CLIP, G_MINUS, G_RATIO, G_LOG, G_Z, G_H, G_SER, G_ART) = range(12)

def build(nc, x, adj, w0, w1, b1, alpha, beta, w_msg, b_msg, w_ih, w_hh, b_ih, b_hh, out, scratch):
    with ExitStack() as ctx:
        def sb(name, shape, dt=F32):
            return ctx.enter_context(nc.sbuf_tensor(name, shape, dt))

        def sem(name):
            return ctx.enter_context(nc.semaphore(name))

        bank = [ctx.enter_context(nc.psum_tensor(f"bank{i}", [P, SLAB], F32)) for i in range(8)]
        strip = bank[:BANKS]
        acc0 = bank[4:8]
        acc, acc_att = bank[4], bank[5]
        rows_a, rows_b = bank[6], bank[7]

        Y = sb("Y", [P, NB, YW], F32R)
        tile = sb("tile", [P, SLABS, Q, SLAB])
        att = sb("att", [P, Q, N])
        unit_h = sb("unit_h", [P, N], F16)
        unit_l = sb("unit_l", [P, N], F16)
        part_h = sb("part_h", [P, BANKS, SLAB], F32R)
        part_l = sb("part_l", [P, BANKS, SLAB], F32R)
        x_nat = att[:, 3, :].rearrange("p (b d) -> p b d", d=D)
        mx = att[:, 2, :].rearrange("p (b d) -> p b d", d=D)
        nat = att[:, 0, 0:Q * YW].rearrange("p (q w) -> p q w", w=YW)

        def spare(n):
            return att[:, 1, SLAB * n:SLAB * (n + 1)]

        def by_block(ap):
            return ap.rearrange("p (q d) -> p q d", d=D)

        ident = sb("ident", [P, P])
        WT = sb("WT", [P, 8, P])
        bias1 = sb("bias1", [P, D])
        turned = sb("turned", [P, SLAB])
        turned_b = sb("turned_b", [P, SLAB])
        t = sb("t", [P, Q, D])
        v = sb("v", [P, Q, D])
        gate_bias = sb("gate_bias", [P, 8])
        half_bias = sb("half_bias", [P, 2])
        power = sb("power", [P, 2, NB])
        half, inv_half = power[:, 0, :], power[:, 1, :]
        dcol = sb("dcol", [P, NB])
        dis = sb("dis", [P, NB])
        d_rows = sb("d_rows", [P, Q])
        sc = sb("sc", [P, 25, Q])
        stats = sb("stats", [P, Q, 6])
        mv = sb("mv", [P, Q, 2])
        peak = sb("peak", [P, Q, SLABS])
        neg_peak = sb("neg_peak", [P, Q])
        exp_sum = sb("exp_sum", [P, Q, 4])
        scal = sb("scal", [P, 7])
        small = spare(3)[:, 0:12 * NB].rearrange("p (k b) -> p k b", b=NB)

        inputs_in = sem("inputs_in")
        consts = sem("consts")
        tile_in = [sem(f"tile_in{c}") for c in range(SLABS)]
        filled = sem("filled")
        bank_read = sem("bank_read")
        hi_done = sem("hi_done")
        product = sem("product")
        acc_read = sem("acc_read")
        row = sem("row")
        y_hi = sem("y_hi")
        y_ready = sem("y_ready")
        y_scaled = sem("y_scaled")
        eye_in = sem("eye_in")
        peaks = sem("peaks")
        exps = sem("exps")
        kept = sem("kept")
        x_back = [sem(f"x_back{g}") for g in range(SLABS)]
        waited = sem("waited")
        dve_link = sem("dve_link")
        pre = sem("pre")
        pre_x = sem("pre_x")
        pre_m = sem("pre_m")
        pre_s = sem("pre_s")
        squared = sem("squared")
        squares_read = sem("squares_read")

        fill_base = [sum(len(FILLS[i]) * SLABS for i in range(l)) for l in range(5)]
        strips = [sum(kind != "S" for kind, _ in FILLS[l]) for l in range(4)]
        strip_base = [sum(strips[i] * SLABS for i in range(l)) for l in range(5)]
        row_base = [sum(len(ROWS[i]) * SLABS for i in range(l)) for l in range(5)]
        acc_reads = [2, 1, 1, 1]
        acc_base = [sum(acc_reads[i] * SLABS for i in range(l)) for l in range(5)]

        def fills(l, s, k):
            return s * len(FILLS[l]) + (fill_base[l] + k + 1)

        def nth_strip(l, k):
            return sum(kind != "S" for kind, _ in FILLS[l][:k])

        def strips_done(l, s, k):
            return s * strips[l] + (strip_base[l] + nth_strip(l, k) + 1)

        def acc_reads_done(l, s):
            return s * acc_reads[l] + (acc_base[l] + acc_reads[l])

        def row_done(l, s, name):
            return s * len(ROWS[l]) + (row_base[l] + ROWS[l].index(name) + 1)

        def row_before(l, s, name):
            return s * len(ROWS[l]) + (row_base[l] + ROWS[l].index(name))

        def last_use(l, j):
            return max(k for k, (kind, i) in enumerate(FILLS[l]) if kind != "S" and i == j)

        def over_slabs(eng, slab):
            for l in range(4):
                slab(l, 0, first=True)
                with eng.Fori(1, SLABS - 1) as s:
                    slab(l, s)
                slab(l, SLABS - 1, last=True)

        def previous(l, s, first):
            return (l - 1, SLABS - 1) if first else (l, s - 1)

        GROUP_AT = [0, 1, 5, 9, 13, 17, 21, 27]

        def groups_at(l, k):
            if l == 2:
                return [g for g in range(SLABS) if k == g]
            return [g for g in range(SLABS) if k == GROUP_AT[g]]

        def wait_apart(eng, semaphore, value):
            eng.wait_ge(semaphore, value)
            if not isinstance(value, int):
                eng.sem_inc(waited, 1)

        block = ctx.enter_context(nc.Block())

        @block.sync
        def _(sp):
            sp.dma_start(x_nat, x.rearrange("(b p) d -> p b d", p=P)).then_inc(inputs_in, 16)
            sp.dma_start(by_block(spare(0))[:, 0, :], w0).then_inc(inputs_in, 16)
            sp.dma_start(t[:, 0, :], w1).then_inc(inputs_in, 16)
            sp.dma_start(t[:, 1, :], w_msg).then_inc(inputs_in, 16)
            sp.dma_start(by_block(spare(1))[:, 0:3, :], w_ih.rearrange("(g p) d -> p g d", p=P)).then_inc(inputs_in, 16)
            sp.dma_start(by_block(spare(2))[:, 0:3, :], w_hh.rearrange("(g p) d -> p g d", p=P)).then_inc(inputs_in, 16)
            sp.dma_start(bias1[:], b1.rearrange("(a d) -> a d", a=1).partition_broadcast(P)).then_inc(inputs_in, 16)
            sp.dma_start(gate_bias[:, 0:1], b_msg.rearrange("(p a) -> p a", a=1)).then_inc(inputs_in, 16)
            for g in range(3):
                sp.dma_start(gate_bias[:, 1 + g:2 + g],
                             b_ih[P * g:P * (g + 1)].rearrange("(p a) -> p a", a=1)).then_inc(inputs_in, 16)
                sp.dma_start(gate_bias[:, 4 + g:5 + g],
                             b_hh[P * g:P * (g + 1)].rearrange("(p a) -> p a", a=1)).then_inc(inputs_in, 16)
            sp.dma_start(scal[:, 0:1], alpha.partition_broadcast(P)).then_inc(inputs_in, 16)
            sp.dma_start(scal[:, 1:2], beta.partition_broadcast(P)).then_inc(inputs_in, 16)

            def slab(l, s, first=False, last=False):
                rows_of = adj[bass.ds(s * SLAB, SLAB), :].rearrange("(q p) j -> p q j", p=P)
                lp, sp_ = previous(l, s, first)
                for c in range(SLABS):
                    if lp >= 0:
                        end = max(k for k, (kind, j) in enumerate(FILLS[lp]) if kind == "A" and j // Q == c)
                        wait_apart(sp, filled, fills(lp, sp_, end))
                        if lp == 2:
                            end = max(k for k, (kind, j) in enumerate(FILLS[lp]) if kind == "S" and j % 8 == c)
                            wait_apart(sp, bank_read, fills(lp, sp_, end) + BANKS)
                    sp.dma_start(tile[:, c, :, :], rows_of[:, :, SLAB * c:SLAB * (c + 1)]).then_inc(tile_in[c], 16)
                if l == 3 and first:
                    for g in range(SLABS):
                        sp.wait_ge(filled, fills(2, SLABS - 1, last_use(2, Q * g + Q - 1)))
                        sp.wait_ge(kept, 16 * (g + 1))
                        sp.dma_start(x_nat[:, Q * g:Q * (g + 1), :],
                                     scratch[SLAB * g:SLAB * (g + 1), :].rearrange("(q p) d -> p q d", p=P)
                                     ).then_inc(x_back[g], 16)

            over_slabs(sp, slab)

        @block.tensor
        def _(pe):
            pe.wait_ge(inputs_in, LOADS * 16)
            pe.wait_ge(consts, 3)
            sources = [t[:, 0, :], t[:, 1, :]] + [by_block(spare(1))[:, g, :] for g in range(3)] \
                + [by_block(spare(2))[:, g, :] for g in range(3)]
            for n, w in enumerate(sources):
                turn = pe.transpose(bank[4 + n // 4][:, P * (n % 4):P * (n % 4 + 1)], w, ident[:])
            turn.then_inc(pre, 1)
            for g in range(SLABS):
                if g == 0:
                    pe.wait_ge(pre, 2)
                else:
                    pe.wait_ge(pre_x, 2 * g)
                for q in range(Q):
                    turn = pe.transpose(bank[4][:, P * q:P * (q + 1)], x_nat[:, Q * g + q, :], ident[:])
                turn.then_inc(pre_x, 1)
                pe.wait_ge(pre_x, 2 * g + 2)
                if g:
                    pe.wait_ge(pre_m, 2 * g)
                for q in range(Q):
                    mm = pe.matmul(bank[5][:, P * q:P * (q + 1)], turned[:, P * q:P * (q + 1)],
                                   by_block(spare(0))[:, 0, :], start=True, stop=True)
                mm.then_inc(pre_m, 1)

            def fill(l, s, k):
                kind, j = FILLS[l][k]
                b = strip[k % BANKS]
                pe.wait_ge(bank_read, fills(l, s, k))
                if kind == "A":
                    if j % Q == 0:
                        pe.wait_ge(tile_in[j // Q], (s + (SLABS * l + 1)) * 16)
                    for q in range(Q):
                        last = pe.transpose(b[:, P * q:P * (q + 1)], tile[:, j // Q, q, P * (j % Q):P * (j % Q + 1)],
                                            ident[:])
                elif kind == "B":
                    if j == 0:
                        pe.wait_ge(exps, s * Q + Q)
                    for q in range(Q):
                        last = pe.transpose(b[:, P * q:P * (q + 1)], att[:, q, P * j:P * (j + 1)], ident[:])
                else:
                    q, c = j // SLABS, j % SLABS
                    mine = bass.ds(s * SLAB + q * P, P)
                    chunk = slice(SLAB * c, SLAB * (c + 1))
                    pe.matmul(b[:], unit_h[:, mine], unit_h[:, chunk], start=True, stop=False)
                    pe.matmul(b[:], unit_h[:, mine], unit_l[:, chunk], start=False, stop=False)
                    last = pe.matmul(b[:], unit_l[:, mine], unit_h[:, chunk], start=False, stop=True)
                last.then_inc(filled, 1)

            def multiply(l, s, k, first):
                kind, j = FILLS[l][k]
                n = nth_strip(l, k) % BANKS
                pe.wait_ge(bank_read, fills(l, s, k) + BANKS)
                if first and j % Q == 0 and kind == "A":
                    pe.wait_ge(y_ready, SLABS * l + j // Q + 1)
                start, stop = j == 0, j == NB - 1
                if l == 0:
                    for q in range(Q):
                        mine = slice(P * q, P * (q + 1))
                        if start:
                            pe.matmul(acc0[q][:, 0:YW], part_h[:, n, mine], Y[:, j, :], start=True, stop=False)
                        last = pe.matmul(acc0[q][:, 0:LO], part_l[:, n, mine], Y[:, j, 0:LO], start=False, stop=False)
                        if not start:
                            last = pe.matmul(acc0[q][:, 0:YW], part_h[:, n, mine], Y[:, j, :], start=False, stop=stop)
                    last.then_inc(product, 1)
                    return
                to = acc_att if kind == "B" else acc
                if l == 1 and stop:
                    pe.wait_ge(eye_in, s + 1)
                    for q in range(Q):
                        mine = slice(P * q, P * (q + 1))
                        pe.matmul(to[:, mine], turned_b[:, mine], ident[:], start=False, stop=False)
                pe.matmul(to[:], Y[:, j, 0:D], part_h[:, n, :], start=start, stop=False)
                pe.matmul(to[:], Y[:, j, LO:LO + D], part_h[:, n, :], start=False, stop=False)
                last = pe.matmul(to[:], Y[:, j, 0:D], part_l[:, n, :], start=False, stop=stop)
                last.then_inc(product, 1)

            def rows1(k, s):
                if k == 4:
                    pe.wait_ge(row, row_before(1, s, "times_w"))
                    pe.wait_ge(acc_read, acc_reads_done(1, s))
                    for q in range(Q):
                        last = pe.matmul(rows_a[:, P * q:P * (q + 1)], turned[:, P * q:P * (q + 1)], WT[:, 0, :],
                                         start=True, stop=True)
                    last.then_inc(row, 1)
                if k == 22:
                    pe.wait_ge(row, row_before(1, s, "turn_unit"))
                    for q in range(Q):
                        last = pe.transpose(rows_b[:, P * q:P * (q + 1)], v[:, q, :], ident[:])
                    last.then_inc(row, 1)

            def rows2(k, s):
                if k == 6:
                    pe.wait_ge(row, row_before(2, s, "turn_back"))
                    pe.wait_ge(acc_read, acc_reads_done(2, s))
                    for q in range(Q):
                        mine = slice(P * q, P * (q + 1))
                        pe.transpose(rows_a[:, mine], turned[:, mine], ident[:])
                        last = pe.transpose(rows_b[:, mine], turned_b[:, mine], ident[:])
                    last.then_inc(row, 1)

            def rows3(k, s):
                if k == 3:
                    pe.wait_ge(row, row_before(3, s, "message"))
                    pe.wait_ge(acc_read, acc_reads_done(3, s))
                    pe.matmul(rows_a[:], WT[:, 1, :], turned[:], start=True, stop=True).then_inc(row, 1)
                if k == 6:
                    pe.wait_ge(row, row_before(3, s, "turn_h"))
                    for q in range(Q):
                        last = pe.transpose(rows_b[:, P * q:P * (q + 1)], t[:, q, :], ident[:])
                    last.then_inc(row, 1)
                if k == 8:
                    pe.wait_ge(row, row_before(3, s, "gate_r"))
                    pe.matmul(rows_a[:], WT[:, 2, :], spare(0), start=True, stop=False)
                    pe.matmul(rows_a[:], WT[:, 5, :], spare(1), start=False, stop=True).then_inc(row, 1)
                if k == 10:
                    pe.wait_ge(row, row_before(3, s, "gate_z"))
                    pe.matmul(rows_b[:], WT[:, 3, :], spare(0), start=True, stop=False)
                    pe.matmul(rows_b[:], WT[:, 6, :], spare(1), start=False, stop=True).then_inc(row, 1)
                if k == 12:
                    pe.wait_ge(row, row_before(3, s, "hidden_n"))
                    pe.matmul(rows_a[:], WT[:, 7, :], spare(1), start=True, stop=True).then_inc(row, 1)
                if k == 14:
                    pe.wait_ge(row, row_before(3, s, "input_n"))
                    pe.matmul(rows_b[:], WT[:, 4, :], spare(0), start=True, stop=True).then_inc(row, 1)
                if k == 20:
                    pe.wait_ge(row, row_before(3, s, "turn_new"))
                    for q in range(Q):
                        last = pe.transpose(rows_a[:, P * q:P * (q + 1)], spare(3)[:, P * q:P * (q + 1)], ident[:])
                    last.then_inc(row, 1)

            rows = [None, rows1, rows2, rows3]

            pe.wait_ge(pre_m, 2 * SLABS)
            for k in range(AHEAD):
                fill(0, 0, k)

            def slab(l, s, first=False, last=False):
                lp, sp_ = previous(l, s, first)
                n = len(FILLS[l])
                if l == 2 and first:
                    for k in range(len(FILLS[1])):
                        rows1(k, sp_)
                for k in range(n):
                    if k + AHEAD < n:
                        fill(l, s, k + AHEAD)
                    elif not last:
                        fill(l, s + 1, k + AHEAD - n)
                    elif l < 3:
                        fill(l + 1, 0, k + AHEAD - n)
                    if k == 0 and lp >= 0:
                        pe.wait_ge(acc_read, acc_reads_done(lp, sp_))
                    if FILLS[l][k][0] != "S":
                        multiply(l, s, k, first)
                    if lp >= 1 and not (l == 2 and first):
                        rows[lp](k, sp_)

            over_slabs(pe, slab)
            for k in range(NB):
                rows3(k, SLABS - 1)

        @block.scalar
        def _(act):
            act.wait_ge(pre, 1)
            act.activation(WT[:, 0:4, :].rearrange("p g d -> p (g d)"), bank[4][:], ACT.Copy)
            act.activation(WT[:, 4:8, :].rearrange("p g d -> p (g d)"), bank[5][:], ACT.Copy).then_inc(pre, 1)
            act.activation(scal[:, 2:3], scal[:, 0:1], ACT.Exp, scale=-1.0).then_inc(pre_s, 1)
            for g in range(SLABS):
                act.wait_ge(pre_x, 2 * g + 1)
                act.activation(turned[:], bank[4][:], ACT.Copy).then_inc(pre_x, 1)
                act.wait_ge(pre_m, 2 * g + 1)
                if g:
                    act.wait_ge(squares_read, g + 1)
                act.activation(turned_b[:], bank[5][:], ACT.Square).then_inc(squared, 1)
                act.activation(mx[:, Q * g:Q * (g + 1), :].rearrange("p q d -> p (q d)"), bank[5][:],
                               ACT.Copy).then_inc(pre_m, 1)
            act.wait_ge(pre, 5)
            act.activation(small[:, G_LOG, :], small[:, G_RATIO, :], ACT.Ln).then_inc(pre, 1)
            act.wait_ge(pre, 7)
            act.activation(small[:, G_H, :], small[:, G_ART, :], ACT.Tanh)
            act.activation(small[:, G_Z, :], small[:, G_ART, :], ACT.Exp, scale=-2.0).then_inc(pre, 1)

            def high(l, s, k):
                kind, j = FILLS[l][k]
                n = nth_strip(l, k) % BANKS
                act.wait_ge(filled, fills(l, s, k))
                act.wait_ge(product, strips_done(l, s, k))
                scale = dis[:, j:j + 1] if l == 2 and kind == "A" else 1.0
                act.activation(part_h[:, n, :], strip[k % BANKS][:], ACT.Copy, scale=scale).then_inc(hi_done, 1)

            def y_high(l, g):
                rows_ = slice(Q * g, Q * (g + 1))
                if l > 0:
                    act.wait_ge(product, strips_done(l - 1, SLABS - 1, last_use(l - 1, Q * g + Q - 1)) + BANKS)
                if l == 0:
                    act.wait_ge(y_scaled, g + 1)
                    source = mx[:, rows_, :]
                elif l == 1:
                    act.wait_ge(y_scaled, SLABS + g + 1)
                    source = mx[:, rows_, :]
                elif l == 2:
                    act.wait_ge(row, row_done(1, g, "ln_out"))
                    source = x_nat[:, rows_, :]
                else:
                    act.wait_ge(x_back[g], 16)
                    source = x_nat[:, rows_, :]
                act.activation(Y[:, rows_, 0:D], source, ACT.Copy).then_inc(y_hi, 1)

            def read_acc(l, s):
                act.wait_ge(product, strips_done(l, s, len(FILLS[l]) - 1) + BANKS)
                if l == 0:
                    act.activation(nat[:, 0, :], acc0[0][:, 0:YW], ACT.Copy)
                    act.activation(nat[:, 1, :], acc0[1][:, 0:YW], ACT.Copy).then_inc(acc_read, 1)
                    return
                if l == 2:
                    act.activation(turned_b[:], acc_att[:], ACT.Copy)
                act.activation(turned[:], acc[:], ACT.Copy).then_inc(acc_read, 1)

            def rows0(k, s):
                if k == 9:
                    act.wait_ge(row, row_before(0, s, "log"))
                    act.activation(sc[:, LOG, :], sc[:, RATIO, :], ACT.Ln).then_inc(row, 1)
                if k == 16:
                    act.wait_ge(row, row_before(0, s, "tanh_u"))
                    act.activation(sc[:, H, :], sc[:, NRM, :], ACT.Tanh).then_inc(row, 1)

            def rows1(k, s):
                if k == 23:
                    act.wait_ge(row, row_before(1, s, "unit_high"))
                    act.activation(unit_h[:, bass.ds(s * SLAB, SLAB)], rows_b[:], ACT.Copy).then_inc(row, 1)

            def rows2(k, s):
                if k == 26:
                    act.wait_ge(row, row_done(2, s, "ln_out"))
                    act.dma_start(scratch[bass.ds(s * SLAB, SLAB), :].rearrange("(q p) d -> p q d", p=P),
                                  v[:]).then_inc(kept, 16)

            def rows3(k, s):
                if k == 4:
                    act.wait_ge(row, row_before(3, s, "message_act"))
                    act.activation(spare(0), rows_a[:], ACT.Relu, bias=gate_bias[:, 0:1]).then_inc(row, 1)
                if k == 7:
                    act.wait_ge(row, row_before(3, s, "h_copy"))
                    act.activation(spare(1), rows_b[:], ACT.Copy).then_inc(row, 1)
                if k == 9:
                    act.wait_ge(row, row_before(3, s, "r_act"))
                    act.activation(spare(2), rows_a[:], ACT.Tanh, scale=0.5, bias=half_bias[:, 0:1]).then_inc(row, 1)
                if k == 11:
                    act.wait_ge(row, row_before(3, s, "z_act"))
                    act.activation(spare(3), rows_b[:], ACT.Tanh, scale=0.5, bias=half_bias[:, 1:2]).then_inc(row, 1)
                if k == 16:
                    act.wait_ge(row, row_before(3, s, "n_act"))
                    act.activation(spare(2), spare(2), ACT.Tanh, bias=gate_bias[:, 3:4]).then_inc(row, 1)
                if k == 27:
                    act.wait_ge(row, row_done(3, s, "ln_out"))
                    act.dma_start(out[bass.ds(s * SLAB, SLAB), :].rearrange("(q p) d -> p q d", p=P),
                                  v[:]).then_inc(kept, 16)

            rows = [rows0, rows1, rows2, rows3]

            def exponentials(s, q, piece, first):
                if piece == 0:
                    act.wait_ge(peaks, s * Q + q + 1)
                    if q == 0 and not first:
                        act.wait_ge(row, row_done(2, s - 1, "sum_exp"))
                mine = att[:, q, N // 4 * piece:N // 4 * (piece + 1)]
                e = act.activation(mine, mine, ACT.Exp, bias=neg_peak[:, q:q + 1],
                                   accum_out=exp_sum[:, q, piece:piece + 1])
                if piece == 3:
                    e.then_inc(exps, 1)

            exp_at = {}
            for q in range(Q):
                end = FILLS[2].index(("S", SLABS * q + SLABS - 1))
                for piece in range(4):
                    exp_at[end + 1 + piece] = (q, piece)

            def slab(l, s, first=False, last=False):
                lp, sp_ = previous(l, s, first)
                if l == 2 and first:
                    read_acc(1, sp_)
                    for k in range(len(FILLS[1])):
                        rows1(k, sp_)
                for k in range(len(FILLS[l])):
                    if k == AHEAD and lp >= 0 and not (l == 2 and first):
                        read_acc(lp, sp_)
                    if first and k == 0 and l == 0:
                        for g in range(SLABS):
                            y_high(0, g)
                    if FILLS[l][k][0] != "S":
                        high(l, s, k)
                    if l == 2 and k in exp_at:
                        exponentials(s, *exp_at[k], first)
                    if first and l > 0:
                        for g in groups_at(l, k):
                            y_high(l, g)
                    if lp >= 0 and not (l == 2 and first):
                        rows[lp](k, sp_)

            over_slabs(act, slab)
            read_acc(3, SLABS - 1)
            for k in range(NB):
                rows3(k, SLABS - 1)
            act.wait_ge(kept, 2 * SLABS * 16)

        @block.gpsimd
        def _(pool):
            pool.memset(ident[:], 0.0).then_inc(consts, 1)
            pool.memset(half, 0.5)
            pool.memset(inv_half, -0.5).then_inc(consts, 1)
            pool.wait_ge(consts, 2)
            pool.affine_select(out=ident[:], in_=ident[:], compare_op=ALU.not_equal, fill=1.0, base=0,
                               pattern=[[-1, P]], channel_multiplier=1).then_inc(consts, 1)
            pool.wait_ge(inputs_in, LOADS * 16)
            everything = att[:, 0, :].rearrange("p (b d) -> p b d", d=D)
            pool.tensor_tensor(everything, x_nat, x_nat, ALU.mult).then_inc(pre_s, 1)
            pool.wait_ge(pre, 3)
            pool.tensor_tensor(small[:, X_N, :], small[:, X_SS, :], half, ALU.pow)
            pool.tensor_tensor(small[:, M_N, :], small[:, M_SS, :], half, ALU.pow).then_inc(pre, 1)

            def y_scale(l, g):
                rows_ = slice(Q * g, Q * (g + 1))
                if l == 0:
                    pool.wait_ge(pre, 9)
                    pool.tensor_tensor(mx[:, rows_, :], mx[:, rows_, :],
                                       small[:, G_SER, rows_].unsqueeze(2).to_broadcast([P, Q, D]),
                                       ALU.mult).then_inc(y_scaled, 1)
                elif l == 1:
                    pool.wait_ge(row, row_done(0, g, "ln_out"))
                    pool.tensor_tensor(mx[:, rows_, :], x_nat[:, rows_, :],
                                       dcol[:, rows_].unsqueeze(2).to_broadcast([P, Q, D]),
                                       ALU.mult).then_inc(y_scaled, 1)

            def y_low(l, g):
                rows_ = slice(Q * g, Q * (g + 1))
                source = mx if l < 2 else x_nat
                pool.wait_ge(y_hi, SLABS * l + g + 1)
                pool.tensor_tensor(Y[:, rows_, LO:LO + D], source[:, rows_, :], Y[:, rows_, 0:D].bitcast(F32),
                                   ALU.subtract).then_inc(y_ready, 1)

            def wide(ap):
                return ap.unsqueeze(2).to_broadcast([P, Q, D])

            def rows0(k, s):
                def before(name):
                    pool.wait_ge(row, row_before(0, s, name))

                def before_apart(name):
                    wait_apart(pool, row, row_before(0, s, name))
                mine = bass.ds(s * Q, Q)
                if k == 3:
                    before("sum_parts")
                    pool.wait_ge(acc_read, acc_reads_done(0, s))
                    pool.tensor_tensor(t[:], nat[:, :, 0:D], nat[:, :, LO:LO + D], ALU.add).then_inc(row, 1)
                    before("sum_den")
                    pool.tensor_tensor(sc[:, DEN, :], nat[:, :, D], nat[:, :, LO + D], ALU.add).then_inc(row, 1)
                    before("square")
                    pool.tensor_tensor(v[:], t[:], t[:], ALU.mult).then_inc(row, 1)
                if k == 6:
                    before("norm")
                    pool.tensor_tensor(sc[:, NRM, :], sc[:, SS, :], half[:, 0:Q], ALU.pow).then_inc(row, 1)
                if k == 11:
                    before("times_scale")
                    pool.tensor_tensor(t[:], t[:], wide(sc[:, SCL, :]), ALU.mult).then_inc(row, 1)
                if k == 13:
                    before("square_u")
                    pool.tensor_tensor(v[:], t[:], t[:], ALU.mult).then_inc(row, 1)
                if k == 15:
                    before("norm_u")
                    pool.tensor_tensor(sc[:, NRM, :], sc[:, SS, :], half[:, 0:Q], ALU.pow).then_inc(row, 1)
                if k == 18:
                    before("times_u")
                    pool.tensor_tensor(t[:], t[:], wide(sc[:, SCL, :]), ALU.mult).then_inc(row, 1)
                    before_apart("add_x")
                    pool.tensor_tensor(t[:], t[:], x_nat[:, mine, :], ALU.add).then_inc(row, 1)
                if k == 20:
                    before("deg_pow")
                    pool.tensor_tensor(sc[:, H, :], sc[:, SAFE, :], inv_half[:, 0:Q], ALU.pow).then_inc(row, 1)
                if k == 22:
                    before_apart("dcol")
                    pool.tensor_tensor(dcol[:, mine], sc[:, H, :], sc[:, ZERO, :], ALU.mult).then_inc(row, 1)
                if k == 24:
                    before_apart("dis")
                    pool.tensor_tensor(dis[:, mine], sc[:, DEG, :], inv_half[:, 0:Q], ALU.pow).then_inc(row, 1)
                if k == 25:
                    layer_norm(0, s)

            def layer_norm(l, s):
                pool.wait_ge(row, row_before(l, s, "ln_rstd"))
                pool.tensor_tensor(sc[:, RSTD, :], sc[:, VAR, :], inv_half[:, 0:Q], ALU.pow).then_inc(row, 1)

            def eye_share(s, first):
                mine = bass.ds(s * Q, Q)
                if not first:
                    wait_apart(pool, product, strips_done(1, s - 1, NB - 1) + BANKS)
                pool.tensor_tensor(by_block(turned_b[:]), x_nat[:, mine, :],
                                   dcol[:, mine].unsqueeze(2).to_broadcast([P, Q, D]), ALU.mult).then_inc(eye_in, 1)

            def rows1(k, s):
                def before(name):
                    pool.wait_ge(row, row_before(1, s, name))

                def before_apart(name):
                    wait_apart(pool, row, row_before(1, s, name))
                mine = bass.ds(s * Q, Q)
                if k == 5:
                    before_apart("x_bias")
                    pool.tensor_tensor(v[:], x_nat[:, mine, :],
                                       bias1[:].unsqueeze(1).to_broadcast([P, Q, D]), ALU.add).then_inc(row, 1)
                    before_apart("d_copy")
                    pool.tensor_copy(d_rows[:], dcol[:, mine]).then_inc(row, 1)
                if k == 10:
                    layer_norm(1, s)
                if k == 14:
                    before_apart("square_x")
                    pool.tensor_tensor(v[:], x_nat[:, mine, :], x_nat[:, mine, :], ALU.mult).then_inc(row, 1)
                if k == 18:
                    before("unit_scale")
                    pool.tensor_tensor(sc[:, H, :], sc[:, SS, :], inv_half[:, 0:Q], ALU.pow).then_inc(row, 1)

            def rows2(k, s):
                def before(name):
                    pool.wait_ge(row, row_before(2, s, name))

                def before_apart(name):
                    wait_apart(pool, row, row_before(2, s, name))
                mine = bass.ds(s * Q, Q)
                if k == 10:
                    before_apart("dis_rows")
                    pool.tensor_copy(sc[:, DEN, :], dis[:, mine]).then_inc(row, 1)
                    before_apart("x_sum")
                    if not isinstance(s, int) or s > 0:
                        wait_apart(pool, kept, s * 16)
                    pool.tensor_tensor(v[:], Y[:, mine, 0:D].bitcast(F32), Y[:, mine, LO:LO + D].bitcast(F32),
                                       ALU.add).then_inc(row, 1)
                if k == 22:
                    layer_norm(2, s)

            def rows3(k, s):
                def before(name):
                    pool.wait_ge(row, row_before(3, s, name))

                def before_apart(name):
                    wait_apart(pool, row, row_before(3, s, name))
                if k == 5:
                    before_apart("stage")
                    pool.tensor_copy(t[:], x_nat[:, bass.ds(s * Q, Q), :]).then_inc(row, 1)
                if k == 17:
                    before_apart("z_half")
                    pool.tensor_scalar(spare(3), spare(3), 1.0, 0.5, ALU.add, ALU.mult).then_inc(row, 1)
                    before("h_minus_n")
                    pool.tensor_tensor(spare(4), spare(1), spare(2), ALU.subtract).then_inc(row, 1)
                    before("z_times")
                    pool.tensor_tensor(spare(4), spare(4), spare(3), ALU.mult).then_inc(row, 1)
                    before("h_new")
                    pool.tensor_tensor(spare(3), spare(4), spare(2), ALU.add).then_inc(row, 1)
                if k == 24:
                    layer_norm(3, s)

            rows = [rows0, rows1, rows2, rows3]

            def slab(l, s, first=False, last=False):
                lp, sp_ = previous(l, s, first)
                if l == 2 and first:
                    for k in range(NB):
                        rows1(k, sp_)
                if l == 1:
                    eye_share(s, first)
                for k in range(len(FILLS[l])):
                    if first:
                        for g in (range(SLABS) if l == 0 and k == 0 else groups_at(l, k) if l else []):
                            y_scale(l, g)
                            y_low(l, g)
                    if lp >= 0 and not (l == 2 and first):
                        rows[lp](k, sp_)

            over_slabs(pool, slab)
            for k in range(NB):
                rows3(k, SLABS - 1)

        @block.vector
        def _(dve):
            linked = [0]

            def link(instruction):
                linked[0] += 1
                instruction.then_inc(dve_link, 1)
                dve.wait_ge(dve_link, linked[0])

            dve.memset(Y[:, :, D + 1:D + 2].bitcast(F32), 1.0)
            dve.memset(Y[:, :, YW - 1:YW].bitcast(F32), 0.0).then_inc(dve_link, 1)
            linked[0] += 1
            dve.wait_ge(inputs_in, LOADS * 16)
            dve.wait_ge(pre_s, 2)
            link(dve.tensor_scalar(scal[:, 3:4], scal[:, 2:3], 1.0, None, ALU.add))
            link(dve.reciprocal(scal[:, 4:5], scal[:, 3:4]))
            dve.tensor_scalar(scal[:, 6:7], scal[:, 4:5], -1.0, None, ALU.mult)
            dve.tensor_scalar(scal[:, 5:6], scal[:, 1:2], 1.0 / XN_SCALE ** 2, None, ALU.mult)
            link(dve.tensor_tensor(half_bias[:], gate_bias[:, 1:3], gate_bias[:, 4:6], ALU.add))
            dve.tensor_scalar(half_bias[:], half_bias[:], 0.5, None, ALU.mult)
            dve.tensor_reduce(small[:, X_SS, :], att[:, 0, :].rearrange("p (b d) -> p b d", d=D), AX.X,
                              ALU.add).then_inc(squares_read, 1)
            for g in range(SLABS):
                dve.wait_ge(squared, g + 1)
                dve.tensor_reduce(small[:, M_SS, Q * g:Q * (g + 1)], by_block(turned_b[:]), AX.X,
                                  ALU.add).then_inc(squares_read, 1)
            dve.wait_ge(squares_read, SLABS + 1)
            dve.tensor_scalar(small[:, X_SS, :], small[:, X_SS, :], MIN_NORM ** 2, None, ALU.max)
            dve.wait_ge(pre, 2)
            dve.tensor_scalar(small[:, M_SS, :], small[:, M_SS, :], MIN_NORM ** 2, None, ALU.max).then_inc(pre, 1)
            dve.wait_ge(pre, 4)
            link(dve.tensor_scalar(small[:, G_CLIP, :], small[:, X_N, :], 1.0 - EPS, None, ALU.min))
            link(dve.tensor_scalar(small[:, G_MINUS, :], small[:, G_CLIP, :], -1.0, 1.0, ALU.mult, ALU.add))
            link(dve.reciprocal(small[:, G_H, :], small[:, G_MINUS, :]))
            dve.scalar_tensor_tensor(small[:, G_RATIO, :], small[:, G_CLIP, :], 1.0, small[:, G_H, :],
                                     ALU.add, ALU.mult).then_inc(pre, 1)
            dve.wait_ge(pre, 5)
            link(dve.tensor_tensor(small[:, G_Z, :], small[:, G_CLIP, :], small[:, G_CLIP, :], ALU.mult))
            link(dve.tensor_scalar(small[:, G_H, :], small[:, G_Z, :], 1.0 / 9, None, ALU.mult))
            for c in (7, 5, 3):
                link(dve.scalar_tensor_tensor(small[:, G_H, :], small[:, G_H, :], 1.0 / c, small[:, G_Z, :],
                                              ALU.add, ALU.mult))
            link(dve.scalar_tensor_tensor(small[:, G_SER, :], small[:, G_H, :], 1.0, small[:, G_CLIP, :],
                                          ALU.add, ALU.mult))
            dve.wait_ge(pre, 6)
            link(dve.scalar_tensor_tensor(small[:, G_SER, :], small[:, G_LOG, :], -0.5, small[:, G_SER, :],
                                          ALU.mult, ALU.add))
            link(dve.scalar_tensor_tensor(small[:, G_SER, :], small[:, G_CLIP, :], TINY_ARTANH, small[:, G_SER, :],
                                          ALU.is_lt, ALU.mult))
            link(dve.scalar_tensor_tensor(small[:, G_ART, :], small[:, G_LOG, :], 0.5, small[:, G_SER, :],
                                          ALU.mult, ALU.add))
            link(dve.reciprocal(small[:, G_Z, :], small[:, X_N, :]))
            link(dve.tensor_tensor(small[:, G_Z, :], small[:, G_Z, :], small[:, M_N, :], ALU.mult))
            dve.tensor_tensor(small[:, G_ART, :], small[:, G_ART, :], small[:, G_Z, :], ALU.mult).then_inc(pre, 1)
            dve.wait_ge(pre, 8)
            link(dve.tensor_scalar(small[:, G_SER, :], small[:, G_Z, :], 1.0, None, ALU.add))
            link(dve.reciprocal(small[:, G_SER, :], small[:, G_SER, :]))
            link(dve.tensor_tensor(small[:, G_SER, :], small[:, G_SER, :], small[:, G_SER, :], ALU.mult))
            link(dve.scalar_tensor_tensor(small[:, G_SER, :], small[:, G_Z, :], 4.0, small[:, G_SER, :],
                                          ALU.mult, ALU.mult))
            link(dve.tensor_scalar(small[:, G_SER, :], small[:, G_SER, :], EPS, None, ALU.max))
            link(dve.reciprocal(small[:, G_SER, :], small[:, G_SER, :]))
            link(dve.tensor_scalar(small[:, G_CLIP, :], small[:, G_SER, :], 2.0, -1.0, ALU.mult, ALU.add))
            dve.tensor_copy(Y[:, :, D], small[:, G_CLIP, :]).then_inc(dve_link, 1)
            linked[0] += 1
            link(dve.reciprocal(small[:, G_RATIO, :], small[:, M_N, :]))
            dve.tensor_tensor(Y[:, :, LO + D], small[:, G_CLIP, :], Y[:, :, D].bitcast(F32), ALU.subtract)
            link(dve.tensor_tensor(small[:, G_RATIO, :], small[:, G_RATIO, :], small[:, G_H, :], ALU.mult))
            dve.scalar_tensor_tensor(small[:, G_SER, :], small[:, G_SER, :], 2.0, small[:, G_RATIO, :],
                                     ALU.mult, ALU.mult).then_inc(pre, 1)
            dve.sem_inc(bank_read, BANKS)
            dve.sem_inc(product, BANKS)

            def read_bank(l, s, k, first):
                kind, j = FILLS[l][k]
                b = strip[k % BANKS]
                if kind == "S":
                    q, c = j // SLABS, j % SLABS
                    if q == 0:
                        wait_apart(dve, tile_in[c], (s + (SLABS * l + 1)) * 16)
                    if first and q == 1 and c == 0:
                        wait_apart(dve, y_ready, SLABS * 3)
                    wait_apart(dve, filled, fills(l, s, k))
                    dve.tensor_tensor_reduce(att[:, q, SLAB * c:SLAB * (c + 1)], b[:], tile[:, c, q, :],
                                             scal[:, 5:6], NEG_HUGE, ALU.mult, ALU.max,
                                             peak[:, q, c:c + 1]).then_inc(bank_read, 1)
                    if c == SLABS - 1:
                        dve.wait_ge(bank_read, fills(l, s, k) + BANKS)
                        dve.tensor_reduce(neg_peak[:, q:q + 1], peak[:, q, :], AX.X, ALU.max,
                                          negate=True).then_inc(peaks, 1)
                    return
                n = nth_strip(l, k) % BANKS
                dve.wait_ge(hi_done, strips_done(l, s, k))
                high = part_h[:, n, :].bitcast(F32)
                if l == 2 and kind == "A":
                    dve.scalar_tensor_tensor(part_l[:, n, :], b[:], dis[:, j:j + 1], high, ALU.mult,
                                             ALU.subtract).then_inc(bank_read, 1)
                else:
                    dve.tensor_tensor(part_l[:, n, :], b[:], high, ALU.subtract).then_inc(bank_read, 1)

            def read_acc(s):
                dve.wait_ge(product, strips_done(0, s, NB - 1) + BANKS)
                dve.tensor_copy(nat[:, 2, :], acc0[2][:, 0:YW])
                dve.tensor_copy(nat[:, 3, :], acc0[3][:, 0:YW]).then_inc(acc_read, 1)

            def layer_norm(l, k, s, to):
                def before(name):
                    dve.wait_ge(row, row_before(l, s, name))

                def before_apart(name):
                    wait_apart(dve, row, row_before(l, s, name))
                if k == 0:
                    before("ln_stats")
                    for q in range(Q):
                        last = dve.bn_stats(stats[:, q, :], t[:, q, :])
                    last.then_inc(row, 1)
                    before_apart("ln_aggr")
                    for q in range(Q):
                        last = dve.bn_aggr(mv[:, q, :], stats[:, q, :])
                    last.then_inc(row, 1)
                    before("ln_eps")
                    dve.tensor_scalar(sc[:, VAR, :], mv[:, :, 1], EPS, None, ALU.add).then_inc(row, 1)
                if k == 1:
                    before("ln_bias")
                    dve.scalar_tensor_tensor(sc[:, BIAS, :], mv[:, :, 0], -1.0, sc[:, RSTD, :], ALU.mult,
                                             ALU.mult).then_inc(row, 1)
                    before("ln_out")
                    for q in range(Q):
                        last = dve.tensor_scalar(to(q), t[:, q, :], sc[:, RSTD, q:q + 1], sc[:, BIAS, q:q + 1],
                                                 ALU.mult, ALU.add)
                    last.then_inc(row, 1)

            def rows0(k, s):
                def before(name):
                    dve.wait_ge(row, row_before(0, s, name))

                def before_apart(name):
                    wait_apart(dve, row, row_before(0, s, name))

                def val(i):
                    return sc[:, i, :]
                if k == 5:
                    before("sum_square")
                    dve.tensor_reduce(val(SS), v[:], AX.X, ALU.add).then_inc(row, 1)
                    before("den_up")
                    dve.tensor_scalar(val(UP), val(DEN), DEN_EPS, None, ALU.max).then_inc(row, 1)
                    before("den_down")
                    dve.tensor_scalar(val(DOWN), val(DEN), -DEN_EPS, None, ALU.min).then_inc(row, 1)
                    before("den_gap")
                    dve.tensor_tensor(val(GAP), val(UP), val(DOWN), ALU.subtract).then_inc(row, 1)
                    before("den_side")
                    dve.scalar_tensor_tensor(val(SIDE), val(DEN), 0.0, val(GAP), ALU.is_ge, ALU.mult).then_inc(row, 1)
                    before("den")
                    dve.tensor_tensor(val(DEN), val(DOWN), val(SIDE), ALU.add).then_inc(row, 1)
                    before("inv_den")
                    dve.reciprocal(val(INV), val(DEN)).then_inc(row, 1)
                    before("inv_den2")
                    dve.tensor_tensor(val(GAP), val(INV), val(INV), ALU.mult).then_inc(row, 1)
                    before("norm2")
                    dve.tensor_tensor(val(SS), val(GAP), val(SS), ALU.mult).then_inc(row, 1)
                if k == 7:
                    before("norm_floor")
                    dve.tensor_scalar(val(NRM), val(NRM), MIN_NORM, None, ALU.max).then_inc(row, 1)
                    before("inv_norm")
                    dve.reciprocal(val(INV_NRM), val(NRM)).then_inc(row, 1)
                    before("clip")
                    dve.tensor_scalar(val(CLIP), val(NRM), 1.0 - EPS, None, ALU.min).then_inc(row, 1)
                    before("one_minus")
                    dve.tensor_scalar(val(MINUS), val(CLIP), -1.0, 1.0, ALU.mult, ALU.add).then_inc(row, 1)
                    before("inv_minus")
                    dve.reciprocal(val(MINUS), val(MINUS)).then_inc(row, 1)
                    before("ratio")
                    dve.scalar_tensor_tensor(val(RATIO), val(CLIP), 1.0, val(MINUS), ALU.add,
                                             ALU.mult).then_inc(row, 1)
                if k == 10:
                    before("z")
                    dve.tensor_tensor(val(Z), val(CLIP), val(CLIP), ALU.mult).then_inc(row, 1)
                    before("h1")
                    dve.tensor_scalar(val(H), val(Z), 1.0 / 9, None, ALU.mult).then_inc(row, 1)
                    for name, c in (("h2", 7), ("h3", 5), ("h4", 3)):
                        before(name)
                        dve.scalar_tensor_tensor(val(H), val(H), 1.0 / c, val(Z), ALU.add, ALU.mult).then_inc(row, 1)
                    before("series")
                    dve.scalar_tensor_tensor(val(SER), val(H), 1.0, val(CLIP), ALU.add, ALU.mult).then_inc(row, 1)
                    before("differ")
                    dve.scalar_tensor_tensor(val(SER), val(LOG), -0.5, val(SER), ALU.mult, ALU.add).then_inc(row, 1)
                    before("choose")
                    dve.scalar_tensor_tensor(val(SER), val(CLIP), TINY_ARTANH, val(SER), ALU.is_lt,
                                             ALU.mult).then_inc(row, 1)
                    before("artanh")
                    dve.scalar_tensor_tensor(val(ART), val(LOG), 0.5, val(SER), ALU.mult, ALU.add).then_inc(row, 1)
                    before("scale")
                    dve.scalar_tensor_tensor(val(SCL), val(ART), 0.5, nat[:, :, D + 1], ALU.mult,
                                             ALU.mult).then_inc(row, 1)
                    before("scale_clip")
                    dve.tensor_scalar(val(SCL), val(SCL), ARTANH_MAX, -ARTANH_MAX, ALU.min, ALU.max).then_inc(row, 1)
                    before("scale_row")
                    dve.tensor_tensor(val(SCL), val(SCL), val(INV), ALU.mult).then_inc(row, 1)
                    before("scale_unit")
                    dve.tensor_tensor(val(SCL), val(SCL), val(INV_NRM), ALU.mult).then_inc(row, 1)
                if k == 12:
                    before("relu")
                    dve.tensor_scalar(t[:], t[:], 0.0, None, ALU.max).then_inc(row, 1)
                if k == 14:
                    before("sum_u")
                    dve.tensor_reduce(val(SS), v[:], AX.X, ALU.add).then_inc(row, 1)
                    before("clamp_u")
                    dve.tensor_scalar(val(SS), val(SS), MIN_NORM ** 2, None, ALU.max).then_inc(row, 1)
                if k == 15:
                    before("inv_u")
                    dve.reciprocal(val(INV), val(NRM)).then_inc(row, 1)
                if k == 17:
                    before("scale_u")
                    dve.tensor_tensor(val(SCL), val(H), val(INV), ALU.mult).then_inc(row, 1)
                if k == 19:
                    before("row_sum")
                    dve.tensor_copy(val(RS), nat[:, :, D + 1]).then_inc(row, 1)
                    before("deg")
                    dve.tensor_scalar(val(DEG), val(RS), 1.0, None, ALU.add).then_inc(row, 1)
                    before("deg_zero")
                    dve.tensor_scalar(val(ZERO), val(DEG), 0.0, None, ALU.is_equal).then_inc(row, 1)
                    before("deg_safe")
                    dve.tensor_tensor(val(SAFE), val(DEG), val(ZERO), ALU.add).then_inc(row, 1)
                if k == 21:
                    before("deg_keep")
                    dve.tensor_scalar(val(ZERO), val(ZERO), -1.0, 1.0, ALU.mult, ALU.add).then_inc(row, 1)
                if k == 23:
                    before("dis_clip")
                    dve.tensor_scalar(val(DEG), val(RS), 1.0, None, ALU.max).then_inc(row, 1)
                if k in (24, 26):
                    layer_norm(0, (k - 24) // 2, s, lambda q: x_nat[:, bass.ds(s * Q + q, 1), :])

            def rows1(k, s):
                def before(name):
                    dve.wait_ge(row, row_before(1, s, name))

                def before_apart(name):
                    wait_apart(dve, row, row_before(1, s, name))
                if k == 7:
                    before("combine")
                    for q in range(Q):
                        last = dve.scalar_tensor_tensor(t[:, q, :], rows_a[:, P * q:P * (q + 1)],
                                                        d_rows[:, q:q + 1], v[:, q, :], ALU.mult, ALU.add)
                    last.then_inc(row, 1)
                if k in (9, 11):
                    layer_norm(1, (k - 9) // 2, s, lambda q: x_nat[:, bass.ds(s * Q + q, 1), :])
                if k == 16:
                    before("sum_x")
                    dve.tensor_reduce(sc[:, SS, :], v[:], AX.X, ALU.add).then_inc(row, 1)
                    before("clamp_x")
                    dve.tensor_scalar(sc[:, SS, :], sc[:, SS, :], COS_EPS ** 2, None, ALU.max).then_inc(row, 1)
                if k == 20:
                    before("unit")
                    for q in range(Q):
                        last = dve.tensor_scalar(v[:, q, :], x_nat[:, bass.ds(s * Q + q, 1), :], sc[:, H, q:q + 1],
                                                 XN_SCALE, ALU.mult, ALU.mult)
                    last.then_inc(row, 1)
                if k == 25:
                    before("unit_low")
                    mine = bass.ds(s * SLAB, SLAB)
                    dve.tensor_tensor(unit_l[:, mine], rows_b[:], unit_h[:, mine], ALU.subtract).then_inc(row, 1)

            def rows2(k, s):
                def before(name):
                    dve.wait_ge(row, row_before(2, s, name))

                def before_apart(name):
                    wait_apart(dve, row, row_before(2, s, name))
                if k == 8:
                    before("sum_exp")
                    dve.tensor_reduce(sc[:, SS, :], exp_sum[:], AX.X, ALU.add).then_inc(row, 1)
                    before("inv_sum")
                    dve.reciprocal(sc[:, INV, :], sc[:, SS, :]).then_inc(row, 1)
                    before("att_scale")
                    dve.tensor_scalar(sc[:, SCL, :], sc[:, INV, :], scal[:, 4:5], None, ALU.mult).then_inc(row, 1)
                if k == 13:
                    before("x_scale")
                    dve.tensor_scalar(v[:], v[:], scal[:, 6:7], None, ALU.mult).then_inc(row, 1)
                if k == 15:
                    before("combine_diff")
                    for q in range(Q):
                        last = dve.scalar_tensor_tensor(t[:, q, :], rows_a[:, P * q:P * (q + 1)],
                                                        sc[:, DEN, q:q + 1], v[:, q, :], ALU.mult, ALU.add)
                    last.then_inc(row, 1)
                if k == 17:
                    before("combine_att")
                    for q in range(Q):
                        last = dve.scalar_tensor_tensor(t[:, q, :], rows_b[:, P * q:P * (q + 1)],
                                                        sc[:, SCL, q:q + 1], t[:, q, :], ALU.mult, ALU.add)
                    last.then_inc(row, 1)
                if k in (20, 24):
                    layer_norm(2, (k - 20) // 4, s, lambda q: v[:, q, :])

            def rows3(k, s):
                def before(name):
                    dve.wait_ge(row, row_before(3, s, name))

                def before_apart(name):
                    wait_apart(dve, row, row_before(3, s, name))
                if k == 13:
                    before("r_half")
                    dve.tensor_scalar(spare(2), spare(2), 1.0, 0.5, ALU.add, ALU.mult).then_inc(row, 1)
                    before("r_times")
                    dve.scalar_tensor_tensor(spare(2), rows_a[:], gate_bias[:, 6:7], spare(2), ALU.add,
                                             ALU.mult).then_inc(row, 1)
                if k == 15:
                    before("n_in")
                    dve.tensor_tensor(spare(2), rows_b[:], spare(2), ALU.add).then_inc(row, 1)
                if k == 21:
                    before("combine")
                    dve.tensor_tensor(t[:].rearrange("p q d -> p (q d)"), rows_a[:],
                                      t[:].rearrange("p q d -> p (q d)"), ALU.add).then_inc(row, 1)
                if k in (23, 25):
                    if k == 25:
                        dve.wait_ge(kept, s * 16 + 16 * SLABS)
                    layer_norm(3, (k - 23) // 2, s, lambda q: v[:, q, :])

            rows = [rows0, rows1, rows2, rows3]

            def slab(l, s, first=False, last=False):
                lp, sp_ = previous(l, s, first)
                if l == 2 and first:
                    for k in range(NB):
                        rows1(k, sp_)
                for k in range(len(FILLS[l])):
                    if k == AHEAD and lp == 0:
                        read_acc(sp_)
                    read_bank(l, s, k, first)
                    if lp >= 0 and not (l == 2 and first):
                        rows[lp](k, sp_)

            over_slabs(dve, slab)
            for k in range(NB):
                rows3(k, SLABS - 1)


_INS = ["x", "adj", "L0_gnn_W", "L1_gnn_W", "L1_gnn_b", "L2_gnn_alpha", "L2_gnn_beta", "L3_gnn_W_msg",
        "L3_gnn_b_msg", "L3_gnn_W_ih", "L3_gnn_W_hh", "L3_gnn_b_ih", "L3_gnn_b_hh"]


def kernel(**inputs):
    import concourse.bacc as bacc
    from concourse.bass_utils import run_bass_kernel_spmd

    nc = bacc.Bacc("TRN2", target_bir_lowering=False, num_devices=1)
    arrays, aps = {}, []
    for name in _INS:
        a = np.ascontiguousarray(inputs[name])
        a = a.reshape(1) if a.ndim == 0 else a
        arrays[f"in_{name}"] = a
        aps.append(nc.dram_tensor(f"in_{name}", a.shape, mybir.dt.from_np(a.dtype), kind="ExternalInput").ap())
    out = nc.dram_tensor("out", (N, D), F32, kind="ExternalOutput").ap()
    scratch = nc.dram_tensor("scratch", (N, D), F32, kind="Internal").ap()
    build(nc, *aps, out, scratch)
    got = run_bass_kernel_spmd(nc, [arrays], core_ids=[0])
    return got.results[0]["out"]
```

```python
from contextlib import ExitStack

import concourse.bass as bass
import numpy as np
from concourse import mybir

F32 = mybir.dt.float32
F32R = mybir.dt.float32r
F16 = mybir.dt.float16
ALU = mybir.AluOpType
ACT = mybir.ActivationFunctionType
AX = mybir.AxisListType

P = 128
N = 4096
D = 128
NB = N // P
Q = 4
SLAB = Q * P
SLABS = N // SLAB
BANKS = 4
AHEAD = 3
YW = 2 * D + 4
LO = D + 2

EPS = 1e-5
MIN_NORM = 1e-15
DEN_EPS = 1e-10
COS_EPS = 1e-8
TINY_ARTANH = 0.125
ARTANH_MAX = float(np.arctanh(np.float32(1.0 - EPS)))
XN_SCALE = 16.0
NEG_HUGE = -3.0e38
LOADS = 14

PLAIN = [("A", j) for j in range(NB)]
ATTEND = []
for _g in range(8):
    for _i in range(4):
        ATTEND.append(("S", 4 * _g + _i))
        if _g or _i == 3:
            ATTEND.append(("A", len(ATTEND) - 4 * _g - _i - 1))
ATTEND += [("A", j) for j in range(29, NB)] + [("B", j) for j in range(NB)]
FILLS = [PLAIN, PLAIN, ATTEND, PLAIN]

LN = ["ln_stats", "ln_aggr", "ln_eps", "ln_rstd", "ln_bias", "ln_out"]
ROWS = [
    ["sum_parts", "sum_den", "degrees", "square", "abs_floor", "inv_abs", "inv_den", "norm", "deg_pow", "norm_den",
     "floor_clip", "artanh_a", "artanh_b", "ratio", "h4", "log", "dcol", "dis", "series", "differ", "choose",
     "artanh", "scale", "scale_clip", "scale_row", "times_relu", "square_u", "clamp_u",
     "norm_u", "tanh_u", "inv_u", "scale_u", "times_u", "add_x"] + LN,
    ["times_w", "x_bias", "d_copy", "combine"] + LN
    + ["square_x", "sum_x", "clamp_x", "unit_scale", "unit", "turn_unit", "unit_high", "unit_low"],
    ["turn_back", "sum_exp", "inv_sum", "att_scale", "dis_rows", "x_sum", "x_scale", "combine_diff",
     "combine_att"] + LN,
    ["message", "message_act", "stage", "turn_h", "h_copy", "gate_r", "r_act", "gate_z", "z_act",
     "hidden_n", "r_half", "r_times", "input_n", "n_in", "n_act", "z_half", "h_minus_n", "z_times", "h_new",
     "turn_new", "combine"] + LN,
]
(DEN, SS, ABS, SIGN, INV_ABS, INV, NRM, INV_NRM, UNIT, CLIP, MINUS, RATIO, LOG, Z, H, SER, ART, SCL, DEG, ZERO,
 KEEP, SAFE, VAR, RSTD, BIAS) = range(25)
(X_SS, M_SS, X_N, M_N, G_CLIP, G_MINUS, G_RATIO, G_LOG, G_Z, G_H, G_SER, G_ART) = range(12)

def build(nc, x, adj, w0, w1, b1, alpha, beta, w_msg, b_msg, w_ih, w_hh, b_ih, b_hh, out, scratch):
    with ExitStack() as ctx:
        def sb(name, shape, dt=F32):
            return ctx.enter_context(nc.sbuf_tensor(name, shape, dt))

        def sem(name):
            return ctx.enter_context(nc.semaphore(name))

        bank = [ctx.enter_context(nc.psum_tensor(f"bank{i}", [P, SLAB], F32)) for i in range(8)]
        strip = bank[:BANKS]
        acc0 = bank[4:8]
        acc, acc_att = bank[4], bank[5]
        rows_a, rows_b = bank[6], bank[7]

        Y = sb("Y", [P, NB, YW], F32R)
        tile = sb("tile", [P, SLABS, Q, SLAB])
        att = sb("att", [P, Q, N])
        unit_h = sb("unit_h", [P, N], F16)
        unit_l = sb("unit_l", [P, N], F16)
        part_h = sb("part_h", [P, BANKS, SLAB], F32R)
        part_l = sb("part_l", [P, BANKS, SLAB], F32R)
        x_nat = att[:, 3, :].rearrange("p (b d) -> p b d", d=D)
        mx = att[:, 2, :].rearrange("p (b d) -> p b d", d=D)
        nat = att[:, 0, 0:Q * YW].rearrange("p (q w) -> p q w", w=YW)

        def spare(n):
            return att[:, 1, SLAB * n:SLAB * (n + 1)]

        def by_block(ap):
            return ap.rearrange("p (q d) -> p q d", d=D)

        ident = sb("ident", [P, P])
        WT = sb("WT", [P, 8, P])
        bias1 = sb("bias1", [P, D])
        turned = sb("turned", [P, SLAB])
        turned_b = sb("turned_b", [P, SLAB])
        t = sb("t", [P, Q, D])
        v = sb("v", [P, Q, D])
        gate_bias = sb("gate_bias", [P, 8])
        half_bias = sb("half_bias", [P, 2])
        power = sb("power", [P, 2, NB])
        half, inv_half = power[:, 0, :], power[:, 1, :]
        dcol = sb("dcol", [P, NB])
        dis = sb("dis", [P, NB])
        d_rows = sb("d_rows", [P, Q])
        sc = sb("sc", [P, 25, Q])
        stats = sb("stats", [P, Q, 6])
        mv = sb("mv", [P, Q, 2])
        peak = sb("peak", [P, Q, SLABS])
        neg_peak = sb("neg_peak", [P, Q])
        exp_sum = sb("exp_sum", [P, Q, 4])
        scal = sb("scal", [P, 7])
        small = spare(3)[:, 0:12 * NB].rearrange("p (k b) -> p k b", b=NB)

        x_in = [sem("x_in0"), sem("x_in1")]
        w0_in = sem("w0_in")
        inputs_in = sem("inputs_in")
        consts = sem("consts")
        tile_in = [sem(f"tile_in{c}") for c in range(SLABS)]
        filled = sem("filled")
        bank_read = sem("bank_read")
        hi_done = sem("hi_done")
        product = sem("product")
        acc_read = sem("acc_read")
        row = sem("row")
        y_hi = sem("y_hi")
        y_ready = sem("y_ready")
        y_scaled = sem("y_scaled")
        eye_in = sem("eye_in")
        peaks = sem("peaks")
        exps = sem("exps")
        kept = sem("kept")
        x_back = [sem(f"x_back{g}") for g in range(SLABS)]
        waited = sem("waited")
        dve_link = sem("dve_link")
        x_ss = sem("x_ss")
        x_norms = sem("x_norms")
        x_turned = sem("x_turned")
        xt_copied = sem("xt_copied")
        m_done = sem("m_done")
        m_copied = sem("m_copied")
        squared = sem("squared")
        squares_read = sem("squares_read")
        m_ss = sem("m_ss")
        m_norms = sem("m_norms")
        ratio_done = sem("ratio_done")
        log_done = sem("log_done")
        u_done = sem("u_done")
        tanh_done = sem("tanh_done")
        y_scales = sem("y_scales")
        w_turned = sem("w_turned")
        w_copied = sem("w_copied")
        exp_alpha = sem("exp_alpha")

        fill_base = [sum(len(FILLS[i]) * SLABS for i in range(l)) for l in range(5)]
        strips = [sum(kind != "S" for kind, _ in FILLS[l]) for l in range(4)]
        strip_base = [sum(strips[i] * SLABS for i in range(l)) for l in range(5)]
        row_base = [sum(len(ROWS[i]) * SLABS for i in range(l)) for l in range(5)]
        acc_reads = [2, 1, 1, 1]
        acc_base = [sum(acc_reads[i] * SLABS for i in range(l)) for l in range(5)]

        def fills(l, s, k):
            return s * len(FILLS[l]) + (fill_base[l] + k + 1)

        def nth_strip(l, k):
            return sum(kind != "S" for kind, _ in FILLS[l][:k])

        def strips_done(l, s, k):
            return s * strips[l] + (strip_base[l] + nth_strip(l, k) + 1)

        def nth_first(l):
            return next(k for k, (kind, _) in enumerate(FILLS[l]) if kind != "S")

        def acc_reads_done(l, s):
            return s * acc_reads[l] + (acc_base[l] + acc_reads[l])

        def row_done(l, s, name):
            return s * len(ROWS[l]) + (row_base[l] + ROWS[l].index(name) + 1)

        def row_before(l, s, name):
            return s * len(ROWS[l]) + (row_base[l] + ROWS[l].index(name))

        def last_use(l, j):
            return max(k for k, (kind, i) in enumerate(FILLS[l]) if kind != "S" and i == j)

        def over_slabs(eng, slab):
            for l in range(4):
                slab(l, 0, first=True)
                with eng.Fori(1, SLABS - 1) as s:
                    slab(l, s)
                slab(l, SLABS - 1, last=True)

        def previous(l, s, first):
            return (l - 1, SLABS - 1) if first else (l, s - 1)

        GROUP_AT = [0, 1, 5, 9, 13, 17, 21, 27]

        def groups_at(l, k):
            if l == 2:
                return [g for g in range(SLABS) if k == g]
            return [g for g in range(SLABS) if k == GROUP_AT[g]]

        def wait_apart(eng, semaphore, value):
            eng.wait_ge(semaphore, value)
            if not isinstance(value, int):
                eng.sem_inc(waited, 1)

        block = ctx.enter_context(nc.Block())

        @block.sync
        def _(sp):
            for h in range(2):
                blocks = slice(NB // 2 * h, NB // 2 * (h + 1))
                sp.dma_start(x_nat[:, blocks, :],
                             x.rearrange("(b p) d -> p b d", p=P)[:, blocks, :]).then_inc(x_in[h], 16)
                if h == 0:
                    sp.dma_start(by_block(spare(0))[:, 0, :], w0).then_inc(w0_in, 16)
            sp.dma_start(t[:, 0, :], w1).then_inc(inputs_in, 16)
            sp.dma_start(t[:, 1, :], w_msg).then_inc(inputs_in, 16)
            sp.dma_start(by_block(spare(1))[:, 0:3, :], w_ih.rearrange("(g p) d -> p g d", p=P)).then_inc(inputs_in, 16)
            sp.dma_start(by_block(spare(2))[:, 0:3, :], w_hh.rearrange("(g p) d -> p g d", p=P)).then_inc(inputs_in, 16)
            sp.dma_start(bias1[:], b1.rearrange("(a d) -> a d", a=1).partition_broadcast(P)).then_inc(inputs_in, 16)
            sp.dma_start(gate_bias[:, 0:1], b_msg.rearrange("(p a) -> p a", a=1)).then_inc(inputs_in, 16)
            for g in range(3):
                sp.dma_start(gate_bias[:, 1 + g:2 + g],
                             b_ih[P * g:P * (g + 1)].rearrange("(p a) -> p a", a=1)).then_inc(inputs_in, 16)
                sp.dma_start(gate_bias[:, 4 + g:5 + g],
                             b_hh[P * g:P * (g + 1)].rearrange("(p a) -> p a", a=1)).then_inc(inputs_in, 16)
            sp.dma_start(scal[:, 0:1], alpha.partition_broadcast(P)).then_inc(inputs_in, 16)
            sp.dma_start(scal[:, 1:2], beta.partition_broadcast(P)).then_inc(inputs_in, 16)

            def slab(l, s, first=False, last=False):
                rows_of = adj[bass.ds(s * SLAB, SLAB), :].rearrange("(q p) j -> p q j", p=P)
                lp, sp_ = previous(l, s, first)
                for c in range(SLABS):
                    if lp >= 0:
                        end = max(k for k, (kind, j) in enumerate(FILLS[lp]) if kind == "A" and j // Q == c)
                        wait_apart(sp, filled, fills(lp, sp_, end))
                        if lp == 2:
                            end = max(k for k, (kind, j) in enumerate(FILLS[lp]) if kind == "S" and j % 8 == c)
                            wait_apart(sp, bank_read, fills(lp, sp_, end) + BANKS)
                    sp.dma_start(tile[:, c, :, :], rows_of[:, :, SLAB * c:SLAB * (c + 1)]).then_inc(tile_in[c], 16)
                if l == 3 and first:
                    for g in range(SLABS):
                        sp.wait_ge(filled, fills(2, SLABS - 1, last_use(2, Q * g + Q - 1)))
                        sp.wait_ge(kept, 16 * (g + 1))
                        sp.dma_start(x_nat[:, Q * g:Q * (g + 1), :],
                                     scratch[SLAB * g:SLAB * (g + 1), :].rearrange("(q p) d -> p q d", p=P)
                                     ).then_inc(x_back[g], 16)

            over_slabs(sp, slab)

        @block.tensor
        def _(pe):
            def turn_x(g):
                pe.wait_ge(x_in[g // 4], 16)
                if g >= 2:
                    pe.wait_ge(xt_copied, g - 1)
                for q in range(Q):
                    turn = pe.transpose(bank[g % 2][:, P * q:P * (q + 1)], x_nat[:, Q * g + q, :], ident[:])
                turn.then_inc(x_turned, 1)

            pe.wait_ge(consts, 3)
            turn_x(0)
            pe.wait_ge(w0_in, 16)
            for g in range(SLABS):
                if g + 1 < SLABS:
                    turn_x(g + 1)
                pe.wait_ge(xt_copied, g + 1)
                if g >= 2:
                    pe.wait_ge(m_copied, g - 1)
                    pe.wait_ge(squared, g - 1)
                rows_of_g = [turned, turned_b][g % 2]
                for q in range(Q):
                    mm = pe.matmul(bank[2 + g % 2][:, P * q:P * (q + 1)], rows_of_g[:, P * q:P * (q + 1)],
                                   by_block(spare(0))[:, 0, :], start=True, stop=True)
                mm.then_inc(m_done, 1)
            pe.wait_ge(inputs_in, LOADS * 16)
            sources = [t[:, 0, :], t[:, 1, :]] + [by_block(spare(1))[:, g, :] for g in range(3)] \
                + [by_block(spare(2))[:, g, :] for g in range(3)]
            for n, w in enumerate(sources):
                turn = pe.transpose(bank[4 + n // 4][:, P * (n % 4):P * (n % 4 + 1)], w, ident[:])
            turn.then_inc(w_turned, 1)

            def fill(l, s, k):
                kind, j = FILLS[l][k]
                b = strip[k % BANKS]
                pe.wait_ge(bank_read, fills(l, s, k))
                if kind == "A":
                    if j % Q == 0:
                        pe.wait_ge(tile_in[j // Q], (s + (SLABS * l + 1)) * 16)
                    for q in range(Q):
                        last = pe.transpose(b[:, P * q:P * (q + 1)], tile[:, j // Q, q, P * (j % Q):P * (j % Q + 1)],
                                            ident[:])
                elif kind == "B":
                    if j % (NB // 4) == 0:
                        pe.wait_ge(exps, s * (4 * Q) + (4 * Q - 3 + j // (NB // 4)))
                    for q in range(Q):
                        last = pe.transpose(b[:, P * q:P * (q + 1)], att[:, q, P * j:P * (j + 1)], ident[:])
                else:
                    q, c = j // SLABS, j % SLABS
                    mine = bass.ds(s * SLAB + q * P, P)
                    chunk = slice(SLAB * c, SLAB * (c + 1))
                    pe.matmul(b[:], unit_h[:, mine], unit_h[:, chunk], start=True, stop=False)
                    pe.matmul(b[:], unit_h[:, mine], unit_l[:, chunk], start=False, stop=False)
                    last = pe.matmul(b[:], unit_l[:, mine], unit_h[:, chunk], start=False, stop=True)
                last.then_inc(filled, 1)

            def multiply(l, s, k, first):
                kind, j = FILLS[l][k]
                n = nth_strip(l, k) % BANKS
                pe.wait_ge(bank_read, fills(l, s, k) + BANKS)
                if first and j % Q == 0 and kind == "A":
                    pe.wait_ge(y_ready, SLABS * l + j // Q + 1)
                start, stop = j == 0, j == NB - 1
                if l == 0:
                    for q in range(Q):
                        mine = slice(P * q, P * (q + 1))
                        if start:
                            pe.matmul(acc0[q][:, 0:YW], part_h[:, n, mine], Y[:, j, :], start=True, stop=False)
                        last = pe.matmul(acc0[q][:, 0:LO], part_l[:, n, mine], Y[:, j, 0:LO], start=False, stop=False)
                        if not start:
                            last = pe.matmul(acc0[q][:, 0:YW], part_h[:, n, mine], Y[:, j, :], start=False, stop=stop)
                    last.then_inc(product, 1)
                    return
                to = acc_att if kind == "B" else acc
                if l == 1 and stop:
                    pe.wait_ge(eye_in, s + 1)
                    for q in range(Q):
                        mine = slice(P * q, P * (q + 1))
                        pe.matmul(to[:, mine], turned_b[:, mine], ident[:], start=False, stop=False)
                pe.matmul(to[:], Y[:, j, 0:D], part_h[:, n, :], start=start, stop=False)
                pe.matmul(to[:], Y[:, j, LO:LO + D], part_h[:, n, :], start=False, stop=False)
                last = pe.matmul(to[:], Y[:, j, 0:D], part_l[:, n, :], start=False, stop=stop)
                last.then_inc(product, 1)

            def rows1(k, s):
                if k == 4:
                    pe.wait_ge(row, row_before(1, s, "times_w"))
                    pe.wait_ge(acc_read, acc_reads_done(1, s))
                    for q in range(Q):
                        last = pe.matmul(rows_a[:, P * q:P * (q + 1)], turned[:, P * q:P * (q + 1)], WT[:, 0, :],
                                         start=True, stop=True)
                    last.then_inc(row, 1)
                if k == 24:
                    pe.wait_ge(row, row_before(1, s, "turn_unit"))
                    for q in range(Q):
                        last = pe.transpose(rows_b[:, P * q:P * (q + 1)], v[:, q, :], ident[:])
                    last.then_inc(row, 1)

            def rows2(k, s):
                if k == 5:
                    pe.wait_ge(row, row_before(2, s, "turn_back"))
                    pe.wait_ge(acc_read, acc_reads_done(2, s))
                    for q in range(Q):
                        mine = slice(P * q, P * (q + 1))
                        pe.transpose(rows_a[:, mine], turned[:, mine], ident[:])
                        last = pe.transpose(rows_b[:, mine], turned_b[:, mine], ident[:])
                    last.then_inc(row, 1)

            def rows3(k, s):
                if k == 3:
                    pe.wait_ge(row, row_before(3, s, "message"))
                    pe.wait_ge(acc_read, acc_reads_done(3, s))
                    pe.matmul(rows_a[:], WT[:, 1, :], turned[:], start=True, stop=True).then_inc(row, 1)
                if k == 6:
                    pe.wait_ge(row, row_before(3, s, "turn_h"))
                    for q in range(Q):
                        last = pe.transpose(rows_b[:, P * q:P * (q + 1)], t[:, q, :], ident[:])
                    last.then_inc(row, 1)
                if k == 8:
                    pe.wait_ge(row, row_before(3, s, "gate_r"))
                    pe.matmul(rows_a[:], WT[:, 2, :], spare(0), start=True, stop=False)
                    pe.matmul(rows_a[:], WT[:, 5, :], spare(1), start=False, stop=True).then_inc(row, 1)
                if k == 10:
                    pe.wait_ge(row, row_before(3, s, "gate_z"))
                    pe.matmul(rows_b[:], WT[:, 3, :], spare(0), start=True, stop=False)
                    pe.matmul(rows_b[:], WT[:, 6, :], spare(1), start=False, stop=True).then_inc(row, 1)
                if k == 12:
                    pe.wait_ge(row, row_before(3, s, "hidden_n"))
                    pe.matmul(rows_a[:], WT[:, 7, :], spare(1), start=True, stop=True).then_inc(row, 1)
                if k == 16:
                    pe.wait_ge(row, row_before(3, s, "input_n"))
                    pe.matmul(rows_b[:], WT[:, 4, :], spare(0), start=True, stop=True).then_inc(row, 1)
                if k == 23:
                    pe.wait_ge(row, row_before(3, s, "turn_new"))
                    for q in range(Q):
                        last = pe.transpose(rows_a[:, P * q:P * (q + 1)], spare(3)[:, P * q:P * (q + 1)], ident[:])
                    last.then_inc(row, 1)

            rows = [None, rows1, rows2, rows3]

            pe.wait_ge(m_copied, SLABS)
            pe.wait_ge(squared, SLABS)
            for k in range(AHEAD):
                fill(0, 0, k)
            pe.wait_ge(w_copied, 1)

            def slab(l, s, first=False, last=False):
                lp, sp_ = previous(l, s, first)
                n = len(FILLS[l])
                if l == 2 and first:
                    for k in range(len(FILLS[1])):
                        rows1(k, sp_)
                for k in range(n):
                    if k + AHEAD < n:
                        fill(l, s, k + AHEAD)
                    elif not last:
                        fill(l, s + 1, k + AHEAD - n)
                    elif l < 3:
                        fill(l + 1, 0, k + AHEAD - n)
                    if k == nth_first(l) and lp >= 0:
                        pe.wait_ge(acc_read, acc_reads_done(lp, sp_))
                    if FILLS[l][k][0] != "S":
                        multiply(l, s, k, first)
                    if lp >= 1 and not (l == 2 and first):
                        rows[lp](k, sp_)

            over_slabs(pe, slab)
            for k in range(NB):
                rows3(k, SLABS - 1)

        @block.scalar
        def _(act):
            def copy_x(g):
                act.wait_ge(x_turned, g + 1)
                if g >= 2:
                    act.wait_ge(m_done, g - 1)
                act.activation([turned, turned_b][g % 2][:], bank[g % 2][:], ACT.Copy).then_inc(xt_copied, 1)

            copy_x(0)
            for g in range(SLABS):
                if g + 1 < SLABS:
                    copy_x(g + 1)
                act.wait_ge(m_done, g + 1)
                act.activation(mx[:, Q * g:Q * (g + 1), :].rearrange("p q d -> p (q d)"), bank[2 + g % 2][:],
                               ACT.Copy).then_inc(m_copied, 1)
                if g >= 2:
                    act.wait_ge(squares_read, g - 1)
                act.activation(spare(4 + g % 2), bank[2 + g % 2][:], ACT.Square).then_inc(squared, 1)
            act.wait_ge(w_turned, 1)
            act.activation(WT[:, 0:4, :].rearrange("p g d -> p (g d)"), bank[4][:], ACT.Copy)
            act.activation(WT[:, 4:8, :].rearrange("p g d -> p (g d)"), bank[5][:], ACT.Copy).then_inc(w_copied, 1)
            act.wait_ge(ratio_done, 1)
            act.activation(small[:, G_LOG, :], small[:, G_RATIO, :], ACT.Ln).then_inc(log_done, 1)
            act.wait_ge(inputs_in, LOADS * 16)
            act.activation(scal[:, 2:3], scal[:, 0:1], ACT.Exp, scale=-1.0).then_inc(exp_alpha, 1)
            act.wait_ge(u_done, 1)
            act.activation(small[:, G_H, :], small[:, G_ART, :], ACT.Tanh)
            act.activation(small[:, G_Z, :], small[:, G_ART, :], ACT.Exp, scale=-2.0).then_inc(tanh_done, 1)

            def high(l, s, k):
                kind, j = FILLS[l][k]
                n = nth_strip(l, k) % BANKS
                act.wait_ge(filled, fills(l, s, k))
                act.wait_ge(product, strips_done(l, s, k))
                scale = dis[:, j:j + 1] if l == 2 and kind == "A" else 1.0
                act.activation(part_h[:, n, :], strip[k % BANKS][:], ACT.Copy, scale=scale).then_inc(hi_done, 1)

            def y_high(l, g):
                rows_ = slice(Q * g, Q * (g + 1))
                if l > 0:
                    act.wait_ge(product, strips_done(l - 1, SLABS - 1, last_use(l - 1, Q * g + Q - 1)) + BANKS)
                if l == 0:
                    act.wait_ge(y_scaled, g + 1)
                    source = mx[:, rows_, :]
                elif l == 1:
                    act.wait_ge(y_scaled, SLABS + g + 1)
                    source = mx[:, rows_, :]
                elif l == 2:
                    act.wait_ge(row, row_done(1, g, "ln_out"))
                    source = x_nat[:, rows_, :]
                else:
                    act.wait_ge(x_back[g], 16)
                    source = x_nat[:, rows_, :]
                act.activation(Y[:, rows_, 0:D], source, ACT.Copy).then_inc(y_hi, 1)

            def read_acc(l, s):
                act.wait_ge(product, strips_done(l, s, len(FILLS[l]) - 1) + BANKS)
                if l == 0:
                    act.activation(nat[:, 0, :], acc0[0][:, 0:YW], ACT.Copy)
                    act.activation(nat[:, 1, :], acc0[1][:, 0:YW], ACT.Copy).then_inc(acc_read, 1)
                    return
                if l == 2:
                    act.activation(turned_b[:], acc_att[:], ACT.Copy)
                act.activation(turned[:], acc[:], ACT.Copy).then_inc(acc_read, 1)

            def rows0(k, s):
                if k == 5:
                    act.wait_ge(row, row_before(0, s, "square"))
                    for q in range(Q):
                        last = act.activation(v[:, q, :], t[:, q, :], ACT.Square, accum_out=sc[:, SS, q:q + 1])
                    last.then_inc(row, 1)
                if k == 11:
                    act.wait_ge(row, row_before(0, s, "log"))
                    act.activation(sc[:, LOG, :], sc[:, RATIO, :], ACT.Ln).then_inc(row, 1)
                if k == 16:
                    act.wait_ge(row, row_before(0, s, "times_relu"))
                    for q in range(Q):
                        last = act.activation(t[:, q, :], t[:, q, :], ACT.Relu, scale=sc[:, SCL, q:q + 1])
                    last.then_inc(row, 1)
                if k == 17:
                    act.wait_ge(row, row_before(0, s, "square_u"))
                    for q in range(Q):
                        last = act.activation(v[:, q, :], t[:, q, :], ACT.Square, accum_out=sc[:, SS, q:q + 1])
                    last.then_inc(row, 1)
                if k == 19:
                    act.wait_ge(row, row_before(0, s, "tanh_u"))
                    act.activation(sc[:, H, :], sc[:, NRM, :], ACT.Tanh).then_inc(row, 1)

            def rows1(k, s):
                if k == 25:
                    act.wait_ge(row, row_before(1, s, "unit_high"))
                    act.activation(unit_h[:, bass.ds(s * SLAB, SLAB)], rows_b[:], ACT.Copy).then_inc(row, 1)

            def rows2(k, s):
                if k == 23:
                    act.wait_ge(row, row_done(2, s, "ln_out"))
                    act.dma_start(scratch[bass.ds(s * SLAB, SLAB), :].rearrange("(q p) d -> p q d", p=P),
                                  v[:]).then_inc(kept, 16)

            def rows3(k, s):
                if k == 4:
                    act.wait_ge(row, row_before(3, s, "message_act"))
                    act.activation(spare(0), rows_a[:], ACT.Relu, bias=gate_bias[:, 0:1]).then_inc(row, 1)
                if k == 7:
                    act.wait_ge(row, row_before(3, s, "h_copy"))
                    act.activation(spare(1), rows_b[:], ACT.Copy).then_inc(row, 1)
                if k == 9:
                    act.wait_ge(row, row_before(3, s, "r_act"))
                    act.activation(spare(2), rows_a[:], ACT.Tanh, scale=0.5, bias=half_bias[:, 0:1]).then_inc(row, 1)
                if k == 11:
                    act.wait_ge(row, row_before(3, s, "z_act"))
                    act.activation(spare(3), rows_b[:], ACT.Tanh, scale=0.5, bias=half_bias[:, 1:2]).then_inc(row, 1)
                if k == 18:
                    act.wait_ge(row, row_before(3, s, "n_act"))
                    act.activation(spare(2), spare(2), ACT.Tanh, bias=gate_bias[:, 3:4]).then_inc(row, 1)
                if k == 30:
                    act.wait_ge(row, row_done(3, s, "ln_out"))
                    act.dma_start(out[bass.ds(s * SLAB, SLAB), :].rearrange("(q p) d -> p q d", p=P),
                                  v[:]).then_inc(kept, 16)

            rows = [rows0, rows1, rows2, rows3]

            def exponentials(s, q, piece, first):
                if piece == 0:
                    act.wait_ge(peaks, s * Q + q + 1)
                    if q == 0 and not first:
                        act.wait_ge(row, row_done(2, s - 1, "sum_exp"))
                mine = att[:, q, N // 4 * piece:N // 4 * (piece + 1)]
                act.activation(mine, mine, ACT.Exp, bias=neg_peak[:, q:q + 1],
                               accum_out=exp_sum[:, q, piece:piece + 1]).then_inc(exps, 1)

            exp_at = {}
            for q in range(Q):
                end = FILLS[2].index(("S", SLABS * q + SLABS - 1))
                for piece in range(4):
                    exp_at[end + 1 + (2 if q == Q - 1 else 3) * piece] = (q, piece)

            def slab(l, s, first=False, last=False):
                lp, sp_ = previous(l, s, first)
                if l == 2 and first:
                    read_acc(1, sp_)
                    for k in range(len(FILLS[1])):
                        rows1(k, sp_)
                for k in range(len(FILLS[l])):
                    if k == AHEAD and lp >= 0 and not (l == 2 and first):
                        read_acc(lp, sp_)
                    if FILLS[l][k][0] != "S":
                        high(l, s, k)
                    if l == 2 and k in exp_at:
                        exponentials(s, *exp_at[k], first)
                    if first:
                        for g in groups_at(l, k):
                            y_high(l, g)
                    if lp >= 0 and not (l == 2 and first):
                        rows[lp](k, sp_)

            over_slabs(act, slab)
            read_acc(3, SLABS - 1)
            for k in range(NB):
                rows3(k, SLABS - 1)
            act.wait_ge(kept, 2 * SLABS * 16)

        @block.gpsimd
        def _(pool):
            pool.memset(ident[:], 0.0).then_inc(consts, 1)
            pool.memset(half, 0.5)
            pool.memset(inv_half, -0.5).then_inc(consts, 1)
            pool.wait_ge(consts, 2)
            pool.affine_select(out=ident[:], in_=ident[:], compare_op=ALU.not_equal, fill=1.0, base=0,
                               pattern=[[-1, P]], channel_multiplier=1).then_inc(consts, 1)
            for h in range(2):
                cols = slice(NB // 2 * h, NB // 2 * (h + 1))
                pool.wait_ge(x_ss, h + 1)
                pool.tensor_tensor(small[:, X_N, cols], small[:, X_SS, cols], half[:, cols], ALU.pow
                                   ).then_inc(x_norms, 1)
            for h in range(2):
                cols = slice(NB // 2 * h, NB // 2 * (h + 1))
                pool.wait_ge(m_ss, h + 1)
                pool.tensor_tensor(small[:, M_N, cols], small[:, M_SS, cols], half[:, cols], ALU.pow
                                   ).then_inc(m_norms, 1)

            def y_scale(l, g):
                rows_ = slice(Q * g, Q * (g + 1))
                if l == 0:
                    pool.wait_ge(y_scales, 1)
                    pool.tensor_tensor(mx[:, rows_, :], mx[:, rows_, :],
                                       small[:, G_SER, rows_].unsqueeze(2).to_broadcast([P, Q, D]),
                                       ALU.mult).then_inc(y_scaled, 1)
                elif l == 1:
                    pool.wait_ge(row, row_done(0, g, "ln_out"))
                    pool.tensor_tensor(mx[:, rows_, :], x_nat[:, rows_, :],
                                       dcol[:, rows_].unsqueeze(2).to_broadcast([P, Q, D]),
                                       ALU.mult).then_inc(y_scaled, 1)

            def y_low(l, g):
                rows_ = slice(Q * g, Q * (g + 1))
                source = mx if l < 2 else x_nat
                pool.wait_ge(y_hi, SLABS * l + g + 1)
                pool.tensor_tensor(Y[:, rows_, LO:LO + D], source[:, rows_, :], Y[:, rows_, 0:D].bitcast(F32),
                                   ALU.subtract).then_inc(y_ready, 1)

            def wide(ap):
                return ap.unsqueeze(2).to_broadcast([P, Q, D])

            def rows0(k, s):
                def before(name):
                    pool.wait_ge(row, row_before(0, s, name))

                def before_apart(name):
                    wait_apart(pool, row, row_before(0, s, name))
                mine = bass.ds(s * Q, Q)
                if k == 3:
                    before("sum_parts")
                    pool.wait_ge(acc_read, acc_reads_done(0, s))
                    pool.tensor_tensor(t[:], nat[:, :, 0:D], nat[:, :, LO:LO + D], ALU.add).then_inc(row, 1)
                    before("sum_den")
                    pool.tensor_tensor(sc[:, DEN, :], nat[:, :, D], nat[:, :, LO + D], ALU.add).then_inc(row, 1)
                if k == 6:
                    before("norm")
                    pool.tensor_tensor(sc[:, NRM, :], sc[:, SS, :], half[:, 0:Q], ALU.pow).then_inc(row, 1)
                    before("deg_pow")
                    pool.tensor_tensor(sc[:, DEG, :], sc[:, SAFE, :], inv_half[:, 0:Q], ALU.pow).then_inc(row, 1)
                if k == 11:
                    before_apart("dcol")
                    pool.tensor_tensor(dcol[:, mine], sc[:, DEG, :], sc[:, KEEP, :], ALU.mult).then_inc(row, 1)
                    before_apart("dis")
                    pool.tensor_tensor(dis[:, mine], sc[:, ZERO, :], inv_half[:, 0:Q], ALU.pow).then_inc(row, 1)
                if k == 18:
                    before("norm_u")
                    pool.tensor_tensor(sc[:, NRM, :], sc[:, SS, :], half[:, 0:Q], ALU.pow).then_inc(row, 1)
                if k == 20:
                    before("times_u")
                    pool.tensor_tensor(t[:], t[:], wide(sc[:, SCL, :]), ALU.mult).then_inc(row, 1)
                    before_apart("add_x")
                    pool.tensor_tensor(t[:], t[:], x_nat[:, mine, :], ALU.add).then_inc(row, 1)
                if k == 24:
                    layer_norm(0, s)

            def layer_norm(l, s):
                pool.wait_ge(row, row_before(l, s, "ln_rstd"))
                pool.tensor_tensor(sc[:, RSTD, :], sc[:, VAR, :], inv_half[:, 0:Q], ALU.pow).then_inc(row, 1)

            def eye_share(s, first):
                mine = bass.ds(s * Q, Q)
                if not first:
                    wait_apart(pool, product, strips_done(1, s - 1, NB - 1) + BANKS)
                pool.tensor_tensor(by_block(turned_b[:]), x_nat[:, mine, :],
                                   dcol[:, mine].unsqueeze(2).to_broadcast([P, Q, D]), ALU.mult).then_inc(eye_in, 1)

            def rows1(k, s):
                def before(name):
                    pool.wait_ge(row, row_before(1, s, name))

                def before_apart(name):
                    wait_apart(pool, row, row_before(1, s, name))
                mine = bass.ds(s * Q, Q)
                if k == 5:
                    before_apart("x_bias")
                    pool.tensor_tensor(v[:], x_nat[:, mine, :],
                                       bias1[:].unsqueeze(1).to_broadcast([P, Q, D]), ALU.add).then_inc(row, 1)
                    before_apart("d_copy")
                    pool.tensor_copy(d_rows[:], dcol[:, mine]).then_inc(row, 1)
                if k == 11:
                    layer_norm(1, s)
                if k == 15:
                    before_apart("square_x")
                    pool.tensor_tensor(v[:], x_nat[:, mine, :], x_nat[:, mine, :], ALU.mult).then_inc(row, 1)
                if k == 18:
                    before("unit_scale")
                    pool.tensor_tensor(sc[:, H, :], sc[:, SS, :], inv_half[:, 0:Q], ALU.pow).then_inc(row, 1)

            def rows2(k, s):
                def before(name):
                    pool.wait_ge(row, row_before(2, s, name))

                def before_apart(name):
                    wait_apart(pool, row, row_before(2, s, name))
                mine = bass.ds(s * Q, Q)
                if k == 8:
                    before_apart("dis_rows")
                    pool.tensor_copy(sc[:, DEN, :], dis[:, mine]).then_inc(row, 1)
                    before_apart("x_sum")
                    if not isinstance(s, int) or s > 0:
                        wait_apart(pool, kept, s * 16)
                    pool.tensor_tensor(v[:], Y[:, mine, 0:D].bitcast(F32), Y[:, mine, LO:LO + D].bitcast(F32),
                                       ALU.add).then_inc(row, 1)
                if k == 19:
                    layer_norm(2, s)

            def rows3(k, s):
                def before(name):
                    pool.wait_ge(row, row_before(3, s, name))

                def before_apart(name):
                    wait_apart(pool, row, row_before(3, s, name))
                if k == 5:
                    before_apart("stage")
                    pool.tensor_copy(t[:], x_nat[:, bass.ds(s * Q, Q), :]).then_inc(row, 1)
                if k == 13:
                    before_apart("r_half")
                    pool.tensor_scalar(spare(2), spare(2), 1.0, 0.5, ALU.add, ALU.mult).then_inc(row, 1)
                if k == 18:
                    before_apart("z_half")
                    pool.tensor_scalar(spare(3), spare(3), 1.0, 0.5, ALU.add, ALU.mult).then_inc(row, 1)
                    before("h_minus_n")
                    pool.tensor_tensor(spare(4), spare(1), spare(2), ALU.subtract).then_inc(row, 1)
                    before("z_times")
                    pool.tensor_tensor(spare(4), spare(4), spare(3), ALU.mult).then_inc(row, 1)
                    before("h_new")
                    pool.tensor_tensor(spare(3), spare(4), spare(2), ALU.add).then_inc(row, 1)
                if k == 26:
                    layer_norm(3, s)

            rows = [rows0, rows1, rows2, rows3]

            def slab(l, s, first=False, last=False):
                lp, sp_ = previous(l, s, first)
                if l == 2 and first:
                    for k in range(NB):
                        rows1(k, sp_)
                if l == 1:
                    eye_share(s, first)
                for k in range(len(FILLS[l])):
                    if first:
                        for g in (range(SLABS) if l == 0 and k == 0 else groups_at(l, k) if l else []):
                            y_scale(l, g)
                            y_low(l, g)
                    if lp >= 0 and not (l == 2 and first):
                        rows[lp](k, sp_)

            over_slabs(pool, slab)
            for k in range(NB):
                rows3(k, SLABS - 1)

        @block.vector
        def _(dve):
            linked = [0]

            def link(instruction):
                linked[0] += 1
                instruction.then_inc(dve_link, 1)
                dve.wait_ge(dve_link, linked[0])

            dve.memset(Y[:, :, D + 1:D + 2].bitcast(F32), 1.0)
            dve.memset(Y[:, :, YW - 1:YW].bitcast(F32), 0.0).then_inc(dve_link, 1)
            linked[0] += 1
            dve.sem_inc(bank_read, BANKS)
            dve.sem_inc(product, BANKS)
            for h in range(2):
                cols = slice(NB // 2 * h, NB // 2 * (h + 1))
                squares = att[:, 0, N // 2 * h:N // 2 * (h + 1)].rearrange("p (b d) -> p b d", d=D)
                dve.wait_ge(x_in[h], 16)
                link(dve.tensor_tensor(squares, x_nat[:, cols, :], x_nat[:, cols, :], ALU.mult))
                link(dve.tensor_reduce(small[:, X_SS, cols], squares, AX.X, ALU.add))
                dve.tensor_scalar(small[:, X_SS, cols], small[:, X_SS, cols], MIN_NORM ** 2, None,
                                  ALU.max).then_inc(x_ss, 1)
            for g in range(SLABS):
                dve.wait_ge(squared, g + 1)
                dve.tensor_reduce(small[:, M_SS, Q * g:Q * (g + 1)], by_block(spare(4 + g % 2)), AX.X,
                                  ALU.add).then_inc(squares_read, 1)
                if g % 4 == 3:
                    cols = slice(NB // 2 * (g // 4), NB // 2 * (g // 4 + 1))
                    dve.wait_ge(squares_read, g + 1)
                    dve.tensor_scalar(small[:, M_SS, cols], small[:, M_SS, cols], MIN_NORM ** 2, None,
                                      ALU.max).then_inc(m_ss, 1)
            dve.wait_ge(x_norms, 2)
            link(dve.tensor_scalar(small[:, G_CLIP, :], small[:, X_N, :], 1.0 - EPS, None, ALU.min))
            link(dve.tensor_scalar(small[:, G_MINUS, :], small[:, G_CLIP, :], -1.0, 1.0, ALU.mult, ALU.add))
            link(dve.reciprocal(small[:, G_H, :], small[:, G_MINUS, :]))
            dve.scalar_tensor_tensor(small[:, G_RATIO, :], small[:, G_CLIP, :], 1.0, small[:, G_H, :],
                                     ALU.add, ALU.mult).then_inc(ratio_done, 1)
            link(dve.tensor_tensor(small[:, G_Z, :], small[:, G_CLIP, :], small[:, G_CLIP, :], ALU.mult))
            link(dve.tensor_scalar(small[:, G_H, :], small[:, G_Z, :], 1.0 / 9, None, ALU.mult))
            for c in (7, 5, 3):
                link(dve.scalar_tensor_tensor(small[:, G_H, :], small[:, G_H, :], 1.0 / c, small[:, G_Z, :],
                                              ALU.add, ALU.mult))
            link(dve.scalar_tensor_tensor(small[:, G_SER, :], small[:, G_H, :], 1.0, small[:, G_CLIP, :],
                                          ALU.add, ALU.mult))
            dve.wait_ge(log_done, 1)
            link(dve.scalar_tensor_tensor(small[:, G_SER, :], small[:, G_LOG, :], -0.5, small[:, G_SER, :],
                                          ALU.mult, ALU.add))
            link(dve.scalar_tensor_tensor(small[:, G_SER, :], small[:, G_CLIP, :], TINY_ARTANH, small[:, G_SER, :],
                                          ALU.is_lt, ALU.mult))
            link(dve.scalar_tensor_tensor(small[:, G_ART, :], small[:, G_LOG, :], 0.5, small[:, G_SER, :],
                                          ALU.mult, ALU.add))
            link(dve.reciprocal(small[:, G_Z, :], small[:, X_N, :]))
            dve.wait_ge(m_norms, 2)
            link(dve.tensor_tensor(small[:, G_Z, :], small[:, G_Z, :], small[:, M_N, :], ALU.mult))
            dve.tensor_tensor(small[:, G_ART, :], small[:, G_ART, :], small[:, G_Z, :], ALU.mult).then_inc(u_done, 1)
            dve.wait_ge(tanh_done, 1)
            link(dve.tensor_scalar(small[:, G_SER, :], small[:, G_Z, :], 1.0, None, ALU.add))
            link(dve.reciprocal(small[:, G_SER, :], small[:, G_SER, :]))
            link(dve.tensor_tensor(small[:, G_SER, :], small[:, G_SER, :], small[:, G_SER, :], ALU.mult))
            link(dve.scalar_tensor_tensor(small[:, G_SER, :], small[:, G_Z, :], 4.0, small[:, G_SER, :],
                                          ALU.mult, ALU.mult))
            link(dve.tensor_scalar(small[:, G_SER, :], small[:, G_SER, :], EPS, None, ALU.max))
            link(dve.reciprocal(small[:, G_SER, :], small[:, G_SER, :]))
            link(dve.tensor_scalar(small[:, G_CLIP, :], small[:, G_SER, :], 2.0, -1.0, ALU.mult, ALU.add))
            dve.tensor_copy(Y[:, :, D], small[:, G_CLIP, :]).then_inc(dve_link, 1)
            linked[0] += 1
            link(dve.reciprocal(small[:, G_RATIO, :], small[:, M_N, :]))
            dve.tensor_tensor(Y[:, :, LO + D], small[:, G_CLIP, :], Y[:, :, D].bitcast(F32), ALU.subtract)
            link(dve.tensor_tensor(small[:, G_RATIO, :], small[:, G_RATIO, :], small[:, G_H, :], ALU.mult))
            dve.scalar_tensor_tensor(small[:, G_SER, :], small[:, G_SER, :], 2.0, small[:, G_RATIO, :],
                                     ALU.mult, ALU.mult).then_inc(y_scales, 1)
            dve.wait_ge(inputs_in, LOADS * 16)
            dve.wait_ge(exp_alpha, 1)
            link(dve.tensor_scalar(scal[:, 3:4], scal[:, 2:3], 1.0, None, ALU.add))
            link(dve.reciprocal(scal[:, 4:5], scal[:, 3:4]))
            dve.tensor_scalar(scal[:, 6:7], scal[:, 4:5], -1.0, None, ALU.mult)
            dve.tensor_scalar(scal[:, 5:6], scal[:, 1:2], 1.0 / XN_SCALE ** 2, None, ALU.mult)
            link(dve.tensor_tensor(half_bias[:], gate_bias[:, 1:3], gate_bias[:, 4:6], ALU.add))
            dve.tensor_scalar(half_bias[:], half_bias[:], 0.5, None, ALU.mult)

            def read_bank(l, s, k, first):
                kind, j = FILLS[l][k]
                b = strip[k % BANKS]
                if kind == "S":
                    q, c = j // SLABS, j % SLABS
                    if q == 0:
                        wait_apart(dve, tile_in[c], (s + (SLABS * l + 1)) * 16)
                    if first and q == 1 and c == 0:
                        wait_apart(dve, y_ready, SLABS * 3)
                    wait_apart(dve, filled, fills(l, s, k))
                    dve.tensor_tensor_reduce(att[:, q, SLAB * c:SLAB * (c + 1)], b[:], tile[:, c, q, :],
                                             scal[:, 5:6], NEG_HUGE, ALU.mult, ALU.max,
                                             peak[:, q, c:c + 1]).then_inc(bank_read, 1)
                    if c == SLABS - 1:
                        dve.wait_ge(bank_read, fills(l, s, k) + BANKS)
                        dve.tensor_reduce(neg_peak[:, q:q + 1], peak[:, q, :], AX.X, ALU.max,
                                          negate=True).then_inc(peaks, 1)
                    return
                n = nth_strip(l, k) % BANKS
                dve.wait_ge(hi_done, strips_done(l, s, k))
                high = part_h[:, n, :].bitcast(F32)
                if l == 2 and kind == "A":
                    dve.scalar_tensor_tensor(part_l[:, n, :], b[:], dis[:, j:j + 1], high, ALU.mult,
                                             ALU.subtract).then_inc(bank_read, 1)
                else:
                    dve.tensor_tensor(part_l[:, n, :], b[:], high, ALU.subtract).then_inc(bank_read, 1)

            def read_acc(s):
                dve.wait_ge(product, strips_done(0, s, NB - 1) + BANKS)
                dve.tensor_copy(nat[:, 2, :], acc0[2][:, 0:YW])
                dve.tensor_copy(nat[:, 3, :], acc0[3][:, 0:YW]).then_inc(acc_read, 1)

            def layer_norm(l, k, s, to):
                def before(name):
                    dve.wait_ge(row, row_before(l, s, name))

                def before_apart(name):
                    wait_apart(dve, row, row_before(l, s, name))
                if k == 0:
                    before("ln_stats")
                    for q in range(Q):
                        last = dve.bn_stats(stats[:, q, :], t[:, q, :])
                    last.then_inc(row, 1)
                if k == 1:
                    before_apart("ln_aggr")
                    for q in range(Q):
                        last = dve.bn_aggr(mv[:, q, :], stats[:, q, :])
                    last.then_inc(row, 1)
                    before("ln_eps")
                    dve.tensor_scalar(sc[:, VAR, :], mv[:, :, 1], EPS, None, ALU.add).then_inc(row, 1)
                if k == 2:
                    before("ln_bias")
                    dve.scalar_tensor_tensor(sc[:, BIAS, :], mv[:, :, 0], -1.0, sc[:, RSTD, :], ALU.mult,
                                             ALU.mult).then_inc(row, 1)
                    before("ln_out")
                if k in (2, 3):
                    for q in (0, 1) if k == 2 else (2, 3):
                        last = dve.tensor_scalar(to(q), t[:, q, :], sc[:, RSTD, q:q + 1], sc[:, BIAS, q:q + 1],
                                                 ALU.mult, ALU.add)
                if k == 3:
                    last.then_inc(row, 1)

            def rows0(k, s):
                def before(name):
                    dve.wait_ge(row, row_before(0, s, name))

                def before_apart(name):
                    wait_apart(dve, row, row_before(0, s, name))

                def val(i):
                    return sc[:, i, :]
                total = nat[:, :, D + 1]
                if k == 5:
                    before("degrees")
                    dve.tensor_scalar(val(Z), total, 1.0, 0.0, ALU.add, ALU.is_equal)
                    dve.tensor_scalar(val(KEEP), total, 1.0, 0.0, ALU.add, ALU.not_equal)
                    dve.tensor_scalar(val(ZERO), total, 1.0, None, ALU.max)
                    dve.scalar_tensor_tensor(val(ABS), val(DEN), -1.0, val(DEN), ALU.mult, ALU.max)
                    dve.tensor_scalar(val(SIGN), val(DEN), 0.0, 2.0, ALU.is_ge, ALU.mult).then_inc(row, 1)
                if k == 6:
                    before("abs_floor")
                    dve.tensor_scalar(val(ABS), val(ABS), DEN_EPS, None, ALU.max).then_inc(row, 1)
                    before("inv_abs")
                    dve.scalar_tensor_tensor(val(SAFE), total, 1.0, val(Z), ALU.add, ALU.add)
                    dve.reciprocal(val(INV_ABS), val(ABS)).then_inc(row, 1)
                    before("inv_den")
                    dve.scalar_tensor_tensor(val(INV), val(SIGN), -1.0, val(INV_ABS), ALU.add,
                                             ALU.mult).then_inc(row, 1)
                if k == 8:
                    before("norm_den")
                    dve.tensor_tensor(val(NRM), val(NRM), val(INV_ABS), ALU.mult).then_inc(row, 1)
                    before("floor_clip")
                    dve.tensor_scalar(val(CLIP), val(NRM), MIN_NORM, 1.0 - EPS, ALU.max, ALU.min)
                    dve.tensor_scalar(val(UNIT), val(NRM), MIN_NORM, None, ALU.max).then_inc(row, 1)
                if k == 9:
                    before("artanh_a")
                    dve.tensor_scalar(val(MINUS), val(CLIP), -1.0, 1.0, ALU.mult, ALU.add)
                    dve.tensor_tensor(val(Z), val(CLIP), val(CLIP), ALU.mult)
                    dve.scalar_tensor_tensor(val(H), val(CLIP), 1.0 / 9, val(CLIP), ALU.mult, ALU.mult)
                    dve.reciprocal(val(INV_NRM), val(UNIT)).then_inc(row, 1)
                    before("artanh_b")
                    dve.reciprocal(val(RATIO), val(MINUS))
                    dve.scalar_tensor_tensor(val(SER), val(H), 1.0 / 7, val(Z), ALU.add, ALU.mult)
                    dve.tensor_tensor(val(UNIT), val(INV), val(INV_NRM), ALU.mult).then_inc(row, 1)
                if k == 10:
                    before("ratio")
                    dve.scalar_tensor_tensor(val(H), val(SER), 1.0 / 5, val(Z), ALU.add, ALU.mult)
                    dve.scalar_tensor_tensor(val(RATIO), val(CLIP), 1.0, val(RATIO), ALU.add,
                                             ALU.mult).then_inc(row, 1)
                    before("h4")
                    dve.scalar_tensor_tensor(val(H), val(H), 1.0 / 3, val(Z), ALU.add, ALU.mult).then_inc(row, 1)
                if k == 12:
                    before("series")
                    dve.scalar_tensor_tensor(val(SER), val(H), 1.0, val(CLIP), ALU.add, ALU.mult).then_inc(row, 1)
                if k == 13:
                    before("differ")
                    dve.scalar_tensor_tensor(val(SER), val(LOG), -0.5, val(SER), ALU.mult, ALU.add).then_inc(row, 1)
                    before("choose")
                    dve.scalar_tensor_tensor(val(SER), val(CLIP), TINY_ARTANH, val(SER), ALU.is_lt,
                                             ALU.mult).then_inc(row, 1)
                if k == 14:
                    before("artanh")
                    dve.scalar_tensor_tensor(val(ART), val(LOG), 0.5, val(SER), ALU.mult, ALU.add).then_inc(row, 1)
                    before("scale")
                    dve.scalar_tensor_tensor(val(SCL), val(ART), 0.5, total, ALU.mult, ALU.mult).then_inc(row, 1)
                if k == 15:
                    before("scale_clip")
                    dve.tensor_scalar(val(SCL), val(SCL), ARTANH_MAX, -ARTANH_MAX, ALU.min, ALU.max).then_inc(row, 1)
                    before("scale_row")
                    dve.tensor_tensor(val(SCL), val(SCL), val(UNIT), ALU.mult).then_inc(row, 1)
                if k == 18:
                    before("clamp_u")
                    dve.tensor_scalar(val(SS), val(SS), MIN_NORM ** 2, None, ALU.max).then_inc(row, 1)
                if k == 20:
                    before("inv_u")
                    dve.reciprocal(val(INV), val(NRM)).then_inc(row, 1)
                    before("scale_u")
                    dve.tensor_tensor(val(SCL), val(H), val(INV), ALU.mult).then_inc(row, 1)
                if k in (22, 23, 25, 26):
                    layer_norm(0, (22, 23, 25, 26).index(k), s, lambda q: x_nat[:, bass.ds(s * Q + q, 1), :])

            def rows1(k, s):
                def before(name):
                    dve.wait_ge(row, row_before(1, s, name))

                def before_apart(name):
                    wait_apart(dve, row, row_before(1, s, name))
                if k in (7, 8):
                    if k == 7:
                        before("combine")
                    for q in (0, 1) if k == 7 else (2, 3):
                        last = dve.scalar_tensor_tensor(t[:, q, :], rows_a[:, P * q:P * (q + 1)],
                                                        d_rows[:, q:q + 1], v[:, q, :], ALU.mult, ALU.add)
                    if k == 8:
                        last.then_inc(row, 1)
                if k in (10, 11, 13, 14):
                    layer_norm(1, (10, 11, 13, 14).index(k), s, lambda q: x_nat[:, bass.ds(s * Q + q, 1), :])
                if k == 17:
                    before("sum_x")
                    dve.tensor_reduce(sc[:, SS, :], v[:], AX.X, ALU.add).then_inc(row, 1)
                if k == 18:
                    before("clamp_x")
                    dve.tensor_scalar(sc[:, SS, :], sc[:, SS, :], COS_EPS ** 2, None, ALU.max).then_inc(row, 1)
                if k in (21, 22):
                    if k == 21:
                        before("unit")
                    for q in (0, 1) if k == 21 else (2, 3):
                        last = dve.tensor_scalar(v[:, q, :], x_nat[:, bass.ds(s * Q + q, 1), :], sc[:, H, q:q + 1],
                                                 XN_SCALE, ALU.mult, ALU.mult)
                    if k == 22:
                        last.then_inc(row, 1)
                if k == 27:
                    before("unit_low")
                    mine = bass.ds(s * SLAB, SLAB)
                    dve.tensor_tensor(unit_l[:, mine], rows_b[:], unit_h[:, mine], ALU.subtract).then_inc(row, 1)

            def rows2(k, s):
                def before(name):
                    dve.wait_ge(row, row_before(2, s, name))

                def before_apart(name):
                    wait_apart(dve, row, row_before(2, s, name))
                if k == 7:
                    before("sum_exp")
                    dve.tensor_reduce(sc[:, SS, :], exp_sum[:], AX.X, ALU.add).then_inc(row, 1)
                    before("inv_sum")
                    dve.reciprocal(sc[:, INV, :], sc[:, SS, :]).then_inc(row, 1)
                    before("att_scale")
                    dve.tensor_scalar(sc[:, SCL, :], sc[:, INV, :], scal[:, 4:5], None, ALU.mult).then_inc(row, 1)
                if k == 11:
                    before("x_scale")
                    dve.tensor_scalar(v[:], v[:], scal[:, 6:7], None, ALU.mult).then_inc(row, 1)
                if k in (12, 14):
                    if k == 12:
                        before("combine_diff")
                    for q in (0, 1) if k == 12 else (2, 3):
                        last = dve.scalar_tensor_tensor(t[:, q, :], rows_a[:, P * q:P * (q + 1)],
                                                        sc[:, DEN, q:q + 1], v[:, q, :], ALU.mult, ALU.add)
                    if k == 14:
                        last.then_inc(row, 1)
                if k in (16, 17):
                    if k == 16:
                        before("combine_att")
                    for q in (0, 1) if k == 16 else (2, 3):
                        last = dve.scalar_tensor_tensor(t[:, q, :], rows_b[:, P * q:P * (q + 1)],
                                                        sc[:, SCL, q:q + 1], t[:, q, :], ALU.mult, ALU.add)
                    if k == 17:
                        last.then_inc(row, 1)
                if k in (18, 19, 21, 22):
                    layer_norm(2, (18, 19, 21, 22).index(k), s, lambda q: v[:, q, :])

            def rows3(k, s):
                def before(name):
                    dve.wait_ge(row, row_before(3, s, name))

                def before_apart(name):
                    wait_apart(dve, row, row_before(3, s, name))
                if k == 14:
                    before("r_times")
                    dve.scalar_tensor_tensor(spare(2), rows_a[:], gate_bias[:, 6:7], spare(2), ALU.add,
                                             ALU.mult).then_inc(row, 1)
                if k == 17:
                    before("n_in")
                    dve.tensor_tensor(spare(2), rows_b[:], spare(2), ALU.add).then_inc(row, 1)
                if k == 24:
                    before("combine")
                    dve.tensor_tensor(t[:].rearrange("p q d -> p (q d)"), rows_a[:],
                                      t[:].rearrange("p q d -> p (q d)"), ALU.add).then_inc(row, 1)
                if k in (25, 26, 28, 29):
                    if k == 28:
                        dve.wait_ge(kept, s * 16 + 16 * SLABS)
                    layer_norm(3, (25, 26, 28, 29).index(k), s, lambda q: v[:, q, :])

            rows = [rows0, rows1, rows2, rows3]

            def slab(l, s, first=False, last=False):
                lp, sp_ = previous(l, s, first)
                if l == 2 and first:
                    for k in range(NB):
                        rows1(k, sp_)
                for k in range(len(FILLS[l])):
                    if k == AHEAD and lp == 0:
                        read_acc(sp_)
                    read_bank(l, s, k, first)
                    if lp >= 0 and not (l == 2 and first):
                        rows[lp](k, sp_)

            over_slabs(dve, slab)
            for k in range(NB):
                rows3(k, SLABS - 1)


_INS = ["x", "adj", "L0_gnn_W", "L1_gnn_W", "L1_gnn_b", "L2_gnn_alpha", "L2_gnn_beta", "L3_gnn_W_msg",
        "L3_gnn_b_msg", "L3_gnn_W_ih", "L3_gnn_W_hh", "L3_gnn_b_ih", "L3_gnn_b_hh"]


def kernel(**inputs):
    import concourse.bacc as bacc
    from concourse.bass_utils import run_bass_kernel_spmd

    nc = bacc.Bacc("TRN2", target_bir_lowering=False, num_devices=1)
    arrays, aps = {}, []
    for name in _INS:
        a = np.ascontiguousarray(inputs[name])
        a = a.reshape(1) if a.ndim == 0 else a
        arrays[f"in_{name}"] = a
        aps.append(nc.dram_tensor(f"in_{name}", a.shape, mybir.dt.from_np(a.dtype), kind="ExternalInput").ap())
    out = nc.dram_tensor("out", (N, D), F32, kind="ExternalOutput").ap()
    scratch = nc.dram_tensor("scratch", (N, D), F32, kind="Internal").ap()
    build(nc, *aps, out, scratch)
    got = run_bass_kernel_spmd(nc, [arrays], core_ids=[0])
    return got.results[0]["out"]
```

```python
from contextlib import ExitStack

import concourse.bass as bass
import numpy as np
from concourse import mybir

F32 = mybir.dt.float32
F32R = mybir.dt.float32r
F16 = mybir.dt.float16
ALU = mybir.AluOpType
ACT = mybir.ActivationFunctionType
AX = mybir.AxisListType

P = 128
N = 4096
D = 128
NB = N // P
Q = 4
SLAB = Q * P
SLABS = N // SLAB
BANKS = 4
AHEAD = 3
YW = 2 * D + 4
LO = D + 2

EPS = 1e-5
MIN_NORM = 1e-15
DEN_EPS = 1e-10
COS_EPS = 1e-8
TINY_ARTANH = 0.125
ARTANH_MAX = float(np.arctanh(np.float32(1.0 - EPS)))
XN_SCALE = 16.0
NEG_HUGE = -3.0e38
LOADS = 14

PLAIN = [("A", j) for j in range(NB)]
SCORES = [("S", i) for i in range(NB)]
WEIGHTS = [("C", j) for j in range(NB)]
SCALE_LATE = 4
BEHIND = 3
BOTH = []
for _j in range(NB):
    BOTH.append(("C", _j))
    if _j >= BEHIND:
        BOTH.append(("S", _j - BEHIND))
BOTH += [("S", i) for i in range(NB - BEHIND, NB)]
STEPS = [SLABS, SLABS, SLABS + 1, SLABS]
WEIGHED_AHEAD = 7
LAST_AHEAD = 2

WEIGH = ["peak", "gap", "shrink", "shrunk_sums", "row_sums", "times_dis", "inverse", "weights"]

LN = ["ln_stats", "ln_aggr", "ln_eps", "ln_rstd", "ln_bias", "ln_out"]
ROWS = [
    ["sum_parts", "sum_den", "degrees", "square", "abs_floor", "inv_abs", "inv_den", "norm", "deg_pow", "norm_den",
     "floor_clip", "artanh_a", "artanh_b", "ratio", "h4", "log", "dcol", "dis", "series", "differ", "choose",
     "artanh", "scale", "scale_clip", "scale_row", "times_relu", "square_u", "clamp_u",
     "norm_u", "tanh_u", "inv_u", "scale_u", "times_u", "add_x"] + LN,
    ["x_bias", "d_copy", "times_w", "combine"] + LN
    + ["square_x", "sum_x", "clamp_x", "unit_scale", "unit", "turn_unit", "unit_high", "unit_low"],
    ["dis_rows", "x_sum", "turn_back", "x_scale", "combine"] + LN,
    ["stage", "turn_h", "message", "h_copy", "message_act", "gate_r", "gate_z", "r_act", "r_half", "z_act", "z_half",
     "hidden_n", "input_n", "r_times", "n_in", "n_act", "h_minus_n", "z_times", "h_new",
     "turn_new", "combine"] + LN,
]
(DEN, SS, ABS, SIGN, INV_ABS, INV, NRM, INV_NRM, UNIT, CLIP, MINUS, RATIO, LOG, Z, H, SER, ART, SCL, DEG, ZERO,
 KEEP, SAFE, VAR, RSTD, BIAS) = range(25)
(X_SS, M_SS, X_N, M_N, G_CLIP, G_MINUS, G_RATIO, G_LOG, G_Z, G_H, G_SER, G_ART) = range(12)

def build(nc, x, adj, w0, w1, b1, alpha, beta, w_msg, b_msg, w_ih, w_hh, b_ih, b_hh, out, scratch, dis_out):
    with ExitStack() as ctx:
        def sb(name, shape, dt=F32):
            return ctx.enter_context(nc.sbuf_tensor(name, shape, dt))

        def sem(name):
            return ctx.enter_context(nc.semaphore(name))

        bank = [ctx.enter_context(nc.psum_tensor(f"bank{i}", [P, SLAB], F32)) for i in range(8)]
        strip = bank[:BANKS]
        acc0 = bank[4:8]
        acc = bank[4]
        rows_a, rows_b = bank[6], bank[7]

        Y = sb("Y", [P, NB, YW], F32R)
        tile = sb("tile", [P, SLABS, Q, SLAB])
        att = sb("att", [P, Q, N])
        unit_h = sb("unit_h", [P, N], F16)
        unit_l = sb("unit_l", [P, N], F16)
        part_h = sb("part_h", [P, BANKS, SLAB], F32R)
        part_l = sb("part_l", [P, BANKS, SLAB], F32R)
        x_nat = att[:, 3, :].rearrange("p (b d) -> p b d", d=D)
        mx = att[:, 2, :].rearrange("p (b d) -> p b d", d=D)
        nat = att[:, 0, 0:Q * YW].rearrange("p (q w) -> p q w", w=YW)

        def spare(n):
            return att[:, 1, SLAB * n:SLAB * (n + 1)]

        def by_block(ap):
            return ap.rearrange("p (q d) -> p q d", d=D)

        ident = sb("ident", [P, P])
        WT = sb("WT", [P, 8, P])
        bias1 = sb("bias1", [P, D])
        turned = sb("turned", [P, SLAB])
        turned_b = sb("turned_b", [P, SLAB])
        dis_row = [turned_b, turned]
        t = sb("t", [P, Q, D])
        v = sb("v", [P, Q, D])
        gate_bias = sb("gate_bias", [P, 8])
        half_bias = sb("half_bias", [P, 2])
        power = sb("power", [P, 2, NB])
        half, inv_half = power[:, 0, :], power[:, 1, :]
        dcol = sb("dcol", [P, NB])
        dis = sb("dis", [P, NB])
        d_rows = sb("d_rows", [P, Q])
        sc = sb("sc", [P, 25, Q])
        stats = sb("stats", [P, Q, 6])
        mv = sb("mv", [P, Q, 2])
        peak = sb("peak", [P, SLABS, Q])
        neg_peak = sb("neg_peak", [P, SLABS, Q])
        exp_sum = sb("exp_sum", [P, SLABS, Q])
        shrink = sb("shrink", [P, SLABS, Q])
        weight = sb("weight", [P, SLABS, Q])
        row_value = sb("row_value", [P, 3, Q])
        own_dis = sb("own_dis", [P, Q])
        scal = sb("scal", [P, 7])
        small = spare(3)[:, 0:12 * NB].rearrange("p (k b) -> p k b", b=NB)

        x_in = [sem("x_in0"), sem("x_in1")]
        w0_in = sem("w0_in")
        inputs_in = sem("inputs_in")
        consts = sem("consts")
        tile_in = [sem(f"tile_in{c}") for c in range(SLABS)]
        filled = sem("filled")
        bank_read = sem("bank_read")
        hi_done = sem("hi_done")
        product = sem("product")
        acc_read = sem("acc_read")
        row = sem("row")
        y_hi = sem("y_hi")
        y_ready = sem("y_ready")
        y_scaled = sem("y_scaled")
        eye_in = sem("eye_in")
        dis_kept = sem("dis_kept")
        dis_row_in = [sem("dis_row_in0"), sem("dis_row_in1")]
        adj_scaled = sem("adj_scaled")
        peaks = sem("peaks")
        exps = sem("exps")
        own_dis_in = sem("own_dis_in")
        weigh = sem("weigh")
        weighed = sem("weighed")
        last_scaled = sem("last_scaled")
        last_weighed = sem("last_weighed")
        kept = sem("kept")
        x_back = [sem(f"x_back{g}") for g in range(SLABS)]
        waited = sem("waited")
        dve_link = sem("dve_link")
        x_ss = sem("x_ss")
        x_norms = sem("x_norms")
        x_turned = sem("x_turned")
        xt_copied = sem("xt_copied")
        m_done = sem("m_done")
        m_copied = sem("m_copied")
        squared = sem("squared")
        squares_read = sem("squares_read")
        m_ss = sem("m_ss")
        m_norms = sem("m_norms")
        ratio_done = sem("ratio_done")
        log_done = sem("log_done")
        u_done = sem("u_done")
        tanh_done = sem("tanh_done")
        y_scales = sem("y_scales")
        w_turned = sem("w_turned")
        w_copied = sem("w_copied")
        exp_alpha = sem("exp_alpha")

        PEAKS = SLABS - 1 + Q
        def fill_list(l, s):
            if l != 2:
                return PLAIN
            if isinstance(s, int) and s in (0, SLABS):
                return SCORES if s == 0 else WEIGHTS
            return BOTH

        def total(l):
            return sum(len(fill_list(l, s)) for s in range(STEPS[l]))

        fill_base = [sum(total(i) for i in range(l)) for l in range(4)]
        row_base = [sum(len(ROWS[i]) * SLABS for i in range(l)) for l in range(4)]
        acc_reads = [2, 1, 1, 1]
        acc_base = [sum(acc_reads[i] * SLABS for i in range(l)) for l in range(4)]

        def fills(l, s, k):
            if l == 2 and not (isinstance(s, int) and s == 0):
                return s * len(BOTH) + (fill_base[l] + len(SCORES) - len(BOTH) + k + 1)
            return s * len(PLAIN) + (fill_base[l] + k + 1)

        def nth_strip(l, s, k):
            return sum(kind in "AC" for kind, _ in fill_list(l, s)[:k])

        def strips_done(l, s, k):
            slab = s - 1 if l == 2 else s
            return slab * NB + (SLABS * NB * l + nth_strip(l, s, k) + 1)

        def slab_done(l, s):
            return s * NB + (SLABS * NB * l + NB)

        def first_strip(l, s):
            return next((k for k, (kind, _) in enumerate(fill_list(l, s)) if kind in "AC"), None)

        def last_at(l, s, k):
            kind, j = fill_list(l, s)[k]
            c = j // Q + LAST_AHEAD
            if kind != "C" or j % Q != Q - 1 or c >= SLABS or isinstance(s, int) and s == 1:
                return []
            return [c]

        def acc_reads_done(l, s):
            return s * acc_reads[l] + (acc_base[l] + acc_reads[l])

        def row_done(l, s, name):
            return s * len(ROWS[l]) + (row_base[l] + ROWS[l].index(name) + 1)

        def row_before(l, s, name):
            return s * len(ROWS[l]) + (row_base[l] + ROWS[l].index(name))

        def weigh_before(s, name):
            return s * len(WEIGH) + WEIGH.index(name)

        def last_use(l, j):
            return SLABS * NB * l + (SLABS - 1) * NB + j + 1

        def over_slabs(eng, step):
            for l in range(4):
                step(l, 0, first=True)
                if l == 2:
                    step(l, 1)
                    step(l, 2)
                with eng.Fori(3 if l == 2 else 1, STEPS[l] - 1) as s:
                    step(l, s)
                step(l, STEPS[l] - 1, last=True)

        def previous(l, s, first):
            if l == 2 and not first:
                return (-1, 0) if isinstance(s, int) and s == 1 else (2, s - 2)
            return (l - 1, SLABS - 1) if first else (l, s - 1)

        GROUP_AT = [0, 1, 5, 9, 13, 17, 21, 27]

        def groups_at(l, k):
            if l == 2:
                return [g for g in range(SLABS) if k == (g if g < SLABS - 1 else 17)]
            return [g for g in range(SLABS) if k == GROUP_AT[g]]

        def wait_apart(eng, semaphore, value):
            eng.wait_ge(semaphore, value)
            if not isinstance(value, int):
                eng.sem_inc(waited, 1)

        block = ctx.enter_context(nc.Block())

        @block.sync
        def _(sp):
            for h in range(2):
                blocks = slice(NB // 2 * h, NB // 2 * (h + 1))
                sp.dma_start(x_nat[:, blocks, :],
                             x.rearrange("(b p) d -> p b d", p=P)[:, blocks, :]).then_inc(x_in[h], 16)
                if h == 0:
                    sp.dma_start(by_block(spare(0))[:, 0, :], w0).then_inc(w0_in, 16)
            sp.dma_start(t[:, 0, :], w1).then_inc(inputs_in, 16)
            sp.dma_start(t[:, 1, :], w_msg).then_inc(inputs_in, 16)
            sp.dma_start(by_block(spare(1))[:, 0:3, :], w_ih.rearrange("(g p) d -> p g d", p=P)).then_inc(inputs_in, 16)
            sp.dma_start(by_block(spare(2))[:, 0:3, :], w_hh.rearrange("(g p) d -> p g d", p=P)).then_inc(inputs_in, 16)
            sp.dma_start(bias1[:], b1.rearrange("(a d) -> a d", a=1).partition_broadcast(P)).then_inc(inputs_in, 16)
            sp.dma_start(gate_bias[:, 0:1], b_msg.rearrange("(p a) -> p a", a=1)).then_inc(inputs_in, 16)
            for g in range(3):
                sp.dma_start(gate_bias[:, 1 + g:2 + g],
                             b_ih[P * g:P * (g + 1)].rearrange("(p a) -> p a", a=1)).then_inc(inputs_in, 16)
                sp.dma_start(gate_bias[:, 4 + g:5 + g],
                             b_hh[P * g:P * (g + 1)].rearrange("(p a) -> p a", a=1)).then_inc(inputs_in, 16)
            sp.dma_start(scal[:, 0:1], alpha.partition_broadcast(P)).then_inc(inputs_in, 16)
            sp.dma_start(scal[:, 1:2], beta.partition_broadcast(P)).then_inc(inputs_in, 16)

            def slab(l, s, first=False, last=False):
                if l == 2 and last:
                    return
                if l == 1 and last:
                    sp.wait_ge(row, row_done(0, SLABS - 1, "dis"))
                    sp.dma_start(dis_out.rearrange("(b p) -> p b", p=P), dis[:], allow_slow_non_contiguous=True).then_inc(dis_kept, 16)
                rows_of = adj[bass.ds(s * SLAB, SLAB), :].rearrange("(q p) j -> p q j", p=P)
                for c in range(SLABS):
                    if l == 2 and not first:
                        wait_apart(sp, weighed, (s - 1) * SLABS + (c + 1))
                        wait_apart(sp, last_weighed, (s - 1) * SLABS + (c + 1))
                    elif l == 3 and first:
                        sp.wait_ge(weighed, (SLABS - 1) * SLABS + (c + 1))
                        sp.wait_ge(last_weighed, (SLABS - 1) * SLABS + (c + 1))
                    elif l > 0 or not first:
                        lp, sp_ = previous(l, s, first)
                        wait_apart(sp, filled, fills(lp, sp_, Q * c + Q - 1))
                    sp.dma_start(tile[:, c, :, :], rows_of[:, :, SLAB * c:SLAB * (c + 1)]).then_inc(tile_in[c], 16)
                    if l == 2:
                        if first and c == 0:
                            sp.wait_ge(dis_kept, 16)
                            sp.wait_ge(product, slab_done(1, SLABS - 1) + BANKS)
                            sp.wait_ge(row, row_done(1, SLABS - 1, "times_w"))
                        if not first or c >= 2:
                            wait_apart(sp, adj_scaled, s * NB + Q * (c - 1))
                        sp.dma_start(dis_row[c % 2][:], dis_out[SLAB * c:SLAB * (c + 1)].rearrange(
                            "(a d) -> a d", a=1).partition_broadcast(P)).then_inc(dis_row_in[c % 2], 16)
                if l == 3 and first:
                    for g in range(SLABS):
                        sp.wait_ge(filled, fills(2, SLABS, WEIGHTS.index(("C", Q * g + Q - 1))))
                        sp.wait_ge(kept, 16 * (g + 1))
                        sp.dma_start(x_nat[:, Q * g:Q * (g + 1), :],
                                     scratch[SLAB * g:SLAB * (g + 1), :].rearrange("(q p) d -> p q d", p=P)
                                     ).then_inc(x_back[g], 16)

            over_slabs(sp, slab)

        @block.tensor
        def _(pe):
            def turn_x(g):
                pe.wait_ge(x_in[g // 4], 16)
                if g >= 2:
                    pe.wait_ge(xt_copied, g - 1)
                for q in range(Q):
                    turn = pe.transpose(bank[g % 2][:, P * q:P * (q + 1)], x_nat[:, Q * g + q, :], ident[:])
                turn.then_inc(x_turned, 1)

            pe.wait_ge(consts, 3)
            turn_x(0)
            pe.wait_ge(w0_in, 16)
            for g in range(SLABS):
                if g + 1 < SLABS:
                    turn_x(g + 1)
                pe.wait_ge(xt_copied, g + 1)
                if g >= 2:
                    pe.wait_ge(m_copied, g - 1)
                    pe.wait_ge(squared, g - 1)
                rows_of_g = [turned, turned_b][g % 2]
                for q in range(Q):
                    mm = pe.matmul(bank[2 + g % 2][:, P * q:P * (q + 1)], rows_of_g[:, P * q:P * (q + 1)],
                                   by_block(spare(0))[:, 0, :], start=True, stop=True)
                mm.then_inc(m_done, 1)
            pe.wait_ge(inputs_in, LOADS * 16)
            sources = [t[:, 0, :], t[:, 1, :]] + [by_block(spare(1))[:, g, :] for g in range(3)] \
                + [by_block(spare(2))[:, g, :] for g in range(3)]
            for n, w in enumerate(sources):
                turn = pe.transpose(bank[4 + n // 4][:, P * (n % 4):P * (n % 4 + 1)], w, ident[:])
            turn.then_inc(w_turned, 1)

            def fill(l, s, k):
                kind, j = fill_list(l, s)[k]
                b = strip[k % BANKS]
                pe.wait_ge(bank_read, fills(l, s, k))
                if kind == "A":
                    if j % Q == 0:
                        pe.wait_ge(tile_in[j // Q], (s + (SLABS * l + 1)) * 16)
                    for q in range(Q):
                        last = pe.transpose(b[:, P * q:P * (q + 1)], tile[:, j // Q, q, P * (j % Q):P * (j % Q + 1)],
                                            ident[:])
                elif kind == "C":
                    c = j // Q
                    if j % Q == 0:
                        pe.wait_ge(weighed, (s - 1) * SLABS + (c + 1))
                        pe.wait_ge(last_weighed, (s - 1) * SLABS + (c + 1))
                    for q in range(Q):
                        last = pe.transpose(b[:, P * q:P * (q + 1)], att[:, q, P * j:P * (j + 1)], ident[:])
                else:
                    c, q = j // Q, j % Q
                    mine = bass.ds(s * SLAB + q * P, P)
                    chunk = slice(SLAB * c, SLAB * (c + 1))
                    if isinstance(s, int) and s == 0 and c == SLABS - 1 and q == 0:
                        pe.wait_ge(row, row_done(1, SLABS - 1, "unit_low"))
                    pe.matmul(b[:], unit_h[:, mine], unit_h[:, chunk], start=True, stop=False)
                    pe.matmul(b[:], unit_h[:, mine], unit_l[:, chunk], start=False, stop=False)
                    last = pe.matmul(b[:], unit_l[:, mine], unit_h[:, chunk], start=False, stop=True)
                last.then_inc(filled, 1)

            def multiply(l, s, k, first):
                kind, j = fill_list(l, s)[k]
                n = nth_strip(l, s, k) % BANKS
                pe.wait_ge(bank_read, fills(l, s, k) + BANKS)
                if first and j % Q == 0:
                    pe.wait_ge(y_ready, SLABS * l + j // Q + 1)
                start, stop = j == 0, j == NB - 1
                if l == 0:
                    for q in range(Q):
                        mine = slice(P * q, P * (q + 1))
                        if start:
                            pe.matmul(acc0[q][:, 0:YW], part_h[:, n, mine], Y[:, j, :], start=True, stop=False)
                        last = pe.matmul(acc0[q][:, 0:LO], part_l[:, n, mine], Y[:, j, 0:LO], start=False, stop=False)
                        if not start:
                            last = pe.matmul(acc0[q][:, 0:YW], part_h[:, n, mine], Y[:, j, :], start=False, stop=stop)
                    last.then_inc(product, 1)
                    return
                to = acc
                if l == 1 and stop:
                    pe.wait_ge(eye_in, s + 1)
                    for q in range(Q):
                        mine = slice(P * q, P * (q + 1))
                        pe.matmul(to[:, mine], turned_b[:, mine], ident[:], start=False, stop=False)
                pe.matmul(to[:], Y[:, j, 0:D], part_h[:, n, :], start=start, stop=False)
                pe.matmul(to[:], Y[:, j, LO:LO + D], part_h[:, n, :], start=False, stop=False)
                last = pe.matmul(to[:], Y[:, j, 0:D], part_l[:, n, :], start=False, stop=stop)
                last.then_inc(product, 1)

            def rows1(k, s):
                if k == 3:
                    pe.wait_ge(row, row_before(1, s, "times_w"))
                    pe.wait_ge(acc_read, acc_reads_done(1, s))
                    for q in range(Q):
                        last = pe.matmul(rows_a[:, P * q:P * (q + 1)], turned[:, P * q:P * (q + 1)], WT[:, 0, :],
                                         start=True, stop=True)
                    last.then_inc(row, 1)
                if k == 21:
                    pe.wait_ge(row, row_before(1, s, "turn_unit"))
                    for q in range(Q):
                        last = pe.transpose(rows_b[:, P * q:P * (q + 1)], v[:, q, :], ident[:])
                    last.then_inc(row, 1)

            def rows2(k, s):
                if k == 4:
                    pe.wait_ge(row, row_before(2, s, "turn_back"))
                    pe.wait_ge(acc_read, acc_reads_done(2, s))
                    for q in range(Q):
                        mine = slice(P * q, P * (q + 1))
                        last = pe.transpose(rows_a[:, mine], t[:, q, :], ident[:])
                    last.then_inc(row, 1)

            def rows3(k, s):
                if k == 1:
                    pe.wait_ge(row, row_before(3, s, "turn_h"))
                    for q in range(Q):
                        last = pe.transpose(rows_b[:, P * q:P * (q + 1)], t[:, q, :], ident[:])
                    last.then_inc(row, 1)
                if k == 2:
                    pe.wait_ge(row, row_before(3, s, "message"))
                    pe.wait_ge(acc_read, acc_reads_done(3, s))
                    pe.matmul(rows_a[:], WT[:, 1, :], turned[:], start=True, stop=True).then_inc(row, 1)
                if k == 5:
                    pe.wait_ge(row, row_before(3, s, "gate_r"))
                    pe.matmul(rows_a[:], WT[:, 2, :], spare(0), start=True, stop=False)
                    pe.matmul(rows_a[:], WT[:, 5, :], spare(1), start=False, stop=True).then_inc(row, 1)
                if k == 7:
                    pe.wait_ge(row, row_before(3, s, "gate_z"))
                    pe.matmul(rows_b[:], WT[:, 3, :], spare(0), start=True, stop=False)
                    pe.matmul(rows_b[:], WT[:, 6, :], spare(1), start=False, stop=True).then_inc(row, 1)
                if k == 12:
                    pe.wait_ge(row, row_before(3, s, "hidden_n"))
                    pe.matmul(rows_a[:], WT[:, 7, :], spare(1), start=True, stop=True).then_inc(row, 1)
                if k == 13:
                    pe.wait_ge(row, row_before(3, s, "input_n"))
                    pe.matmul(rows_b[:], WT[:, 4, :], spare(0), start=True, stop=True).then_inc(row, 1)
                if k == 22:
                    pe.wait_ge(row, row_before(3, s, "turn_new"))
                    for q in range(Q):
                        last = pe.transpose(rows_a[:, P * q:P * (q + 1)], spare(3)[:, P * q:P * (q + 1)], ident[:])
                    last.then_inc(row, 1)

            rows = [None, rows1, rows2, rows3]

            pe.wait_ge(m_copied, SLABS)
            pe.wait_ge(squared, SLABS)
            for k in range(AHEAD):
                fill(0, 0, k)
            pe.wait_ge(w_copied, 1)

            def slab(l, s, first=False, last=False):
                lp, sp_ = previous(l, s, first)
                n = len(fill_list(l, s))
                for k in range(n):
                    if k + AHEAD < n:
                        fill(l, s, k + AHEAD)
                    elif not last:
                        fill(l, s + 1, k + AHEAD - n)
                    elif l < 3:
                        fill(l + 1, 0, k + AHEAD - n)
                    if k == first_strip(l, s) and lp >= 0:
                        pe.wait_ge(acc_read, acc_reads_done(lp, sp_))
                    if l == 2 and k == 0 and isinstance(s, int) and s == 1:
                        pe.wait_ge(y_ready, SLABS * 3)
                    if fill_list(l, s)[k][0] != "S":
                        multiply(l, s, k, first)
                    if lp >= 1:
                        rows[lp](k, sp_)

            over_slabs(pe, slab)
            for k in range(NB):
                rows3(k, SLABS - 1)

        @block.scalar
        def _(act):
            def copy_x(g):
                act.wait_ge(x_turned, g + 1)
                if g >= 2:
                    act.wait_ge(m_done, g - 1)
                act.activation([turned, turned_b][g % 2][:], bank[g % 2][:], ACT.Copy).then_inc(xt_copied, 1)

            copy_x(0)
            for g in range(SLABS):
                if g + 1 < SLABS:
                    copy_x(g + 1)
                act.wait_ge(m_done, g + 1)
                act.activation(mx[:, Q * g:Q * (g + 1), :].rearrange("p q d -> p (q d)"), bank[2 + g % 2][:],
                               ACT.Copy).then_inc(m_copied, 1)
                if g >= 2:
                    act.wait_ge(squares_read, g - 1)
                act.activation(spare(4 + g % 2), bank[2 + g % 2][:], ACT.Square).then_inc(squared, 1)
            act.wait_ge(w_turned, 1)
            act.activation(WT[:, 0:4, :].rearrange("p g d -> p (g d)"), bank[4][:], ACT.Copy)
            act.activation(WT[:, 4:8, :].rearrange("p g d -> p (g d)"), bank[5][:], ACT.Copy).then_inc(w_copied, 1)
            act.wait_ge(ratio_done, 1)
            act.activation(small[:, G_LOG, :], small[:, G_RATIO, :], ACT.Ln).then_inc(log_done, 1)
            act.wait_ge(inputs_in, LOADS * 16)
            act.activation(scal[:, 2:3], scal[:, 0:1], ACT.Exp, scale=-1.0).then_inc(exp_alpha, 1)
            act.wait_ge(u_done, 1)
            act.activation(small[:, G_H, :], small[:, G_ART, :], ACT.Tanh)
            act.activation(small[:, G_Z, :], small[:, G_ART, :], ACT.Exp, scale=-2.0).then_inc(tanh_done, 1)

            def high(l, s, k):
                kind, j = fill_list(l, s)[k]
                n = nth_strip(l, s, k) % BANKS
                act.wait_ge(filled, fills(l, s, k))
                act.wait_ge(product, strips_done(l, s, k))
                act.activation(part_h[:, n, :], strip[k % BANKS][:], ACT.Copy).then_inc(hi_done, 1)

            def y_high(l, g):
                rows_ = slice(Q * g, Q * (g + 1))
                if l > 0:
                    act.wait_ge(product, last_use(l - 1, Q * g + Q - 1) + BANKS)
                if l == 0:
                    act.wait_ge(y_scaled, g + 1)
                    source = mx[:, rows_, :]
                elif l == 1:
                    act.wait_ge(y_scaled, SLABS + g + 1)
                    source = mx[:, rows_, :]
                elif l == 2:
                    act.wait_ge(row, row_done(1, g, "ln_out"))
                    source = x_nat[:, rows_, :]
                else:
                    act.wait_ge(x_back[g], 16)
                    source = x_nat[:, rows_, :]
                act.activation(Y[:, rows_, 0:D], source, ACT.Copy).then_inc(y_hi, 1)

            def read_acc(l, s):
                act.wait_ge(product, slab_done(l, s) + BANKS)
                if l == 0:
                    act.activation(nat[:, 0, :], acc0[0][:, 0:YW], ACT.Copy)
                    act.activation(nat[:, 1, :], acc0[1][:, 0:YW], ACT.Copy).then_inc(acc_read, 1)
                    return
                to = t[:].rearrange("p q d -> p (q d)") if l == 2 else turned[:]
                act.activation(to, acc[:], ACT.Copy).then_inc(acc_read, 1)

            def rows0(k, s):
                if k == 5:
                    act.wait_ge(row, row_before(0, s, "square"))
                    for q in range(Q):
                        last = act.activation(v[:, q, :], t[:, q, :], ACT.Square, accum_out=sc[:, SS, q:q + 1])
                    last.then_inc(row, 1)
                if k == 11:
                    act.wait_ge(row, row_before(0, s, "log"))
                    act.activation(sc[:, LOG, :], sc[:, RATIO, :], ACT.Ln).then_inc(row, 1)
                if k == 16:
                    act.wait_ge(row, row_before(0, s, "times_relu"))
                    for q in range(Q):
                        last = act.activation(t[:, q, :], t[:, q, :], ACT.Relu, scale=sc[:, SCL, q:q + 1])
                    last.then_inc(row, 1)
                if k == 17:
                    act.wait_ge(row, row_before(0, s, "square_u"))
                    for q in range(Q):
                        last = act.activation(v[:, q, :], t[:, q, :], ACT.Square, accum_out=sc[:, SS, q:q + 1])
                    last.then_inc(row, 1)
                if k == 19:
                    act.wait_ge(row, row_before(0, s, "tanh_u"))
                    act.activation(sc[:, H, :], sc[:, NRM, :], ACT.Tanh).then_inc(row, 1)

            def rows1(k, s):
                if k == 25:
                    act.wait_ge(row, row_before(1, s, "unit_high"))
                    act.activation(unit_h[:, bass.ds(s * SLAB, SLAB)], rows_b[:], ACT.Copy).then_inc(row, 1)

            def rows2(k, s):
                if k == 23:
                    act.wait_ge(row, row_done(2, s, "ln_out"))
                    act.dma_start(scratch[bass.ds(s * SLAB, SLAB), :].rearrange("(q p) d -> p q d", p=P),
                                  v[:]).then_inc(kept, 16)

            def rows3(k, s):
                if k == 6:
                    act.wait_ge(row, row_before(3, s, "h_copy"))
                    act.activation(spare(1), rows_b[:], ACT.Copy).then_inc(row, 1)
                if k == 7:
                    act.wait_ge(row, row_before(3, s, "message_act"))
                    act.activation(spare(0), rows_a[:], ACT.Relu, bias=gate_bias[:, 0:1]).then_inc(row, 1)
                if k == 11:
                    act.wait_ge(row, row_before(3, s, "r_act"))
                    act.activation(spare(2), rows_a[:], ACT.Tanh, scale=0.5, bias=half_bias[:, 0:1]).then_inc(row, 1)
                if k == 13:
                    act.wait_ge(row, row_before(3, s, "z_act"))
                    act.activation(spare(3), rows_b[:], ACT.Tanh, scale=0.5, bias=half_bias[:, 1:2]).then_inc(row, 1)
                if k == 20:
                    act.wait_ge(row, row_before(3, s, "n_act"))
                    act.activation(spare(2), spare(2), ACT.Tanh, bias=gate_bias[:, 3:4]).then_inc(row, 1)
                if k == 31:
                    act.wait_ge(row, row_done(3, s, "ln_out"))
                    act.dma_start(out[bass.ds(s * SLAB, SLAB), :].rearrange("(q p) d -> p q d", p=P),
                                  v[:]).then_inc(kept, 16)

            rows = [rows0, rows1, rows2, rows3]

            def exponentials(s, i):
                c, q = i // Q, i % Q
                if q == 0 or c == SLABS - 1:
                    act.wait_ge(peaks, s * PEAKS + (c + 1 + (q if c == SLABS - 1 else 0)))
                mine = att[:, q, SLAB * c:SLAB * (c + 1)]
                e = act.activation(mine, mine, ACT.Exp, bias=neg_peak[:, c, q:q + 1],
                                   accum_out=exp_sum[:, c, q:q + 1])
                if q == Q - 1:
                    e.then_inc(exps, 1)

            def scale_last(c):
                mine = att[:, Q - 1, SLAB * c:SLAB * (c + 1)]
                act.activation(mine, mine, ACT.Copy, scale=weight[:, c, Q - 1:Q]).then_inc(last_scaled, 1)

            def exps_at(s):
                kinds = fill_list(2, s)
                at = [[] for _ in kinds]
                for i in range(NB if ("S", 0) in kinds else 0):
                    end = kinds.index(("S", i // Q * Q + Q - 1))
                    apart = 2 if kinds is BOTH and i // Q < SLABS - 2 else 1
                    at[min(end + 1 + apart * (i % Q), len(kinds) - 1)].append(i)
                return at

            def slab(l, s, first=False, last=False):
                lp, sp_ = previous(l, s, first)
                for k in range(len(fill_list(l, s))):
                    if k == AHEAD and lp >= 0:
                        read_acc(lp, sp_)
                    if fill_list(l, s)[k][0] != "S":
                        high(l, s, k)
                    for c in last_at(l, s, k):
                        scale_last(c)
                    if first:
                        for g in groups_at(l, k):
                            y_high(l, g)
                    if l == 2:
                        for i in exps_at(s)[k]:
                            exponentials(s, i)
                    if lp >= 0:
                        rows[lp](k, sp_)
                if l == 2 and not last:
                    act.wait_ge(weigh, weigh_before(s, "shrink"))
                    act.activation(shrink[:], shrink[:], ACT.Exp).then_inc(weigh, 1)
                    if not first:
                        act.wait_ge(weigh, weigh_before(s + 1, "peak"))
                        for c in range(LAST_AHEAD):
                            scale_last(c)

            over_slabs(act, slab)
            read_acc(3, SLABS - 1)
            for k in range(NB):
                rows3(k, SLABS - 1)
            act.wait_ge(kept, 2 * SLABS * 16)

        @block.gpsimd
        def _(pool):
            pool.memset(ident[:], 0.0).then_inc(consts, 1)
            pool.memset(half, 0.5)
            pool.memset(inv_half, -0.5).then_inc(consts, 1)
            pool.wait_ge(consts, 2)
            pool.affine_select(out=ident[:], in_=ident[:], compare_op=ALU.not_equal, fill=1.0, base=0,
                               pattern=[[-1, P]], channel_multiplier=1).then_inc(consts, 1)
            for h in range(2):
                cols = slice(NB // 2 * h, NB // 2 * (h + 1))
                pool.wait_ge(x_ss, h + 1)
                pool.tensor_tensor(small[:, X_N, cols], small[:, X_SS, cols], half[:, cols], ALU.pow
                                   ).then_inc(x_norms, 1)
            for h in range(2):
                cols = slice(NB // 2 * h, NB // 2 * (h + 1))
                pool.wait_ge(m_ss, h + 1)
                pool.tensor_tensor(small[:, M_N, cols], small[:, M_SS, cols], half[:, cols], ALU.pow
                                   ).then_inc(m_norms, 1)

            def y_scale(l, g):
                rows_ = slice(Q * g, Q * (g + 1))
                if l == 0:
                    pool.wait_ge(y_scales, 1)
                    pool.tensor_tensor(mx[:, rows_, :], mx[:, rows_, :],
                                       small[:, G_SER, rows_].unsqueeze(2).to_broadcast([P, Q, D]),
                                       ALU.mult).then_inc(y_scaled, 1)
                elif l == 1:
                    pool.wait_ge(row, row_done(0, g, "ln_out"))
                    pool.tensor_tensor(mx[:, rows_, :], x_nat[:, rows_, :],
                                       dcol[:, rows_].unsqueeze(2).to_broadcast([P, Q, D]),
                                       ALU.mult).then_inc(y_scaled, 1)

            def y_low(l, g):
                rows_ = slice(Q * g, Q * (g + 1))
                source = mx if l < 2 else x_nat
                pool.wait_ge(y_hi, SLABS * l + g + 1)
                pool.tensor_tensor(Y[:, rows_, LO:LO + D], source[:, rows_, :], Y[:, rows_, 0:D].bitcast(F32),
                                   ALU.subtract).then_inc(y_ready, 1)

            def wide(ap):
                return ap.unsqueeze(2).to_broadcast([P, Q, D])

            def rows0(k, s):
                def before(name):
                    pool.wait_ge(row, row_before(0, s, name))

                def before_apart(name):
                    wait_apart(pool, row, row_before(0, s, name))
                mine = bass.ds(s * Q, Q)
                if k == 3:
                    before("sum_parts")
                    pool.wait_ge(acc_read, acc_reads_done(0, s))
                    pool.tensor_tensor(t[:], nat[:, :, 0:D], nat[:, :, LO:LO + D], ALU.add).then_inc(row, 1)
                    before("sum_den")
                    pool.tensor_tensor(sc[:, DEN, :], nat[:, :, D], nat[:, :, LO + D], ALU.add).then_inc(row, 1)
                if k == 6:
                    before("norm")
                    pool.tensor_tensor(sc[:, NRM, :], sc[:, SS, :], half[:, 0:Q], ALU.pow).then_inc(row, 1)
                    before("deg_pow")
                    pool.tensor_tensor(sc[:, DEG, :], sc[:, SAFE, :], inv_half[:, 0:Q], ALU.pow).then_inc(row, 1)
                if k == 11:
                    before_apart("dcol")
                    pool.tensor_tensor(dcol[:, mine], sc[:, DEG, :], sc[:, KEEP, :], ALU.mult).then_inc(row, 1)
                    before_apart("dis")
                    pool.tensor_tensor(dis[:, mine], sc[:, ZERO, :], inv_half[:, 0:Q], ALU.pow).then_inc(row, 1)
                if k == 18:
                    before("norm_u")
                    pool.tensor_tensor(sc[:, NRM, :], sc[:, SS, :], half[:, 0:Q], ALU.pow).then_inc(row, 1)
                if k == 20:
                    before("times_u")
                    pool.tensor_tensor(t[:], t[:], wide(sc[:, SCL, :]), ALU.mult).then_inc(row, 1)
                    before_apart("add_x")
                    pool.tensor_tensor(t[:], t[:], x_nat[:, mine, :], ALU.add).then_inc(row, 1)
                if k == 24:
                    layer_norm(0, s)

            def layer_norm(l, s):
                pool.wait_ge(row, row_before(l, s, "ln_rstd"))
                pool.tensor_tensor(sc[:, RSTD, :], sc[:, VAR, :], inv_half[:, 0:Q], ALU.pow).then_inc(row, 1)

            def eye_share(s, first):
                mine = bass.ds(s * Q, Q)
                if not first:
                    wait_apart(pool, product, slab_done(1, s - 1) + BANKS)
                pool.tensor_tensor(by_block(turned_b[:]), x_nat[:, mine, :],
                                   dcol[:, mine].unsqueeze(2).to_broadcast([P, Q, D]), ALU.mult).then_inc(eye_in, 1)

            def rows1(k, s):
                def before(name):
                    pool.wait_ge(row, row_before(1, s, name))

                def before_apart(name):
                    wait_apart(pool, row, row_before(1, s, name))
                mine = bass.ds(s * Q, Q)
                if k == 1:
                    before_apart("x_bias")
                    pool.tensor_tensor(v[:], x_nat[:, mine, :],
                                       bias1[:].unsqueeze(1).to_broadcast([P, Q, D]), ALU.add).then_inc(row, 1)
                    before_apart("d_copy")
                    pool.tensor_copy(d_rows[:], dcol[:, mine]).then_inc(row, 1)
                if k == 11:
                    layer_norm(1, s)
                if k == 15:
                    before_apart("square_x")
                    pool.tensor_tensor(v[:], x_nat[:, mine, :], x_nat[:, mine, :], ALU.mult).then_inc(row, 1)
                if k == 18:
                    before("unit_scale")
                    pool.tensor_tensor(sc[:, H, :], sc[:, SS, :], inv_half[:, 0:Q], ALU.pow).then_inc(row, 1)

            def rows2(k, s):
                def before(name):
                    pool.wait_ge(row, row_before(2, s, name))

                def before_apart(name):
                    wait_apart(pool, row, row_before(2, s, name))
                mine = bass.ds(s * Q, Q)
                if k == 1:
                    before_apart("dis_rows")
                    pool.tensor_copy(sc[:, DEN, :], dis[:, mine]).then_inc(row, 1)
                    before_apart("x_sum")
                    if not isinstance(s, int) or s > 0:
                        wait_apart(pool, kept, s * 16)
                    pool.tensor_tensor(v[:], Y[:, mine, 0:D].bitcast(F32), Y[:, mine, LO:LO + D].bitcast(F32),
                                       ALU.add).then_inc(row, 1)
                if k == 19:
                    layer_norm(2, s)

            def rows3(k, s):
                def before(name):
                    pool.wait_ge(row, row_before(3, s, name))

                def before_apart(name):
                    wait_apart(pool, row, row_before(3, s, name))
                if k == 1:
                    before_apart("stage")
                    pool.tensor_copy(t[:], x_nat[:, bass.ds(s * Q, Q), :]).then_inc(row, 1)
                if k == 12:
                    before_apart("r_half")
                    pool.tensor_scalar(spare(2), spare(2), 1.0, 0.5, ALU.add, ALU.mult).then_inc(row, 1)
                if k == 14:
                    before_apart("z_half")
                    pool.tensor_scalar(spare(3), spare(3), 1.0, 0.5, ALU.add, ALU.mult).then_inc(row, 1)
                if k == 20:
                    before("h_minus_n")
                    pool.tensor_tensor(spare(4), spare(1), spare(2), ALU.subtract).then_inc(row, 1)
                    before("z_times")
                    pool.tensor_tensor(spare(4), spare(4), spare(3), ALU.mult).then_inc(row, 1)
                    before("h_new")
                    pool.tensor_tensor(spare(3), spare(4), spare(2), ALU.add).then_inc(row, 1)
                if k == 28:
                    layer_norm(3, s)

            rows = [rows0, rows1, rows2, rows3]

            def sum_last(s, c):
                mine = att[:, Q - 1, SLAB * c:SLAB * (c + 1)]
                pool.wait_ge(last_scaled, (s - 1) * SLABS + (c + 1))
                pool.tensor_tensor(mine, mine, tile[:, c, Q - 1, :], ALU.add).then_inc(last_weighed, 1)

            def scale_block(s, k):
                c, q = fill_list(2, s)[k][1] // Q, fill_list(2, s)[k][1] % Q
                if q == 0:
                    pool.wait_ge(dis_row_in[c % 2], s * (16 * SLABS // 2) + 16 * (c // 2 + 1))
                pool.wait_ge(bank_read, fills(2, s, k) + BANKS)
                pool.tensor_tensor(tile[:, c, q, :], tile[:, c, q, :], dis_row[c % 2][:],
                                   ALU.mult).then_inc(adj_scaled, 1)

            def slab(l, s, first=False, last=False):
                lp, sp_ = previous(l, s, first)
                if l == 1:
                    eye_share(s, first)
                if l == 2 and not last:
                    if not first:
                        wait_apart(pool, weigh, weigh_before(s, "peak"))
                    pool.tensor_copy(own_dis[:], dis[:, bass.ds(s * Q, Q)]).then_inc(own_dis_in, 1)
                for k in range(len(fill_list(l, s))):
                    if first:
                        for g in (range(SLABS) if l == 0 and k == 0 else groups_at(l, k) if l else []):
                            y_scale(l, g)
                            y_low(l, g)
                    if lp >= 0:
                        rows[lp](k, sp_)
                    late = SCALE_LATE if first else 0
                    if l == 2 and k >= late and fill_list(l, s)[k - late][0] == "S":
                        scale_block(s, k - late)
                    for c in last_at(l, s, k):
                        sum_last(s - 1, c)
                if l == 2 and first:
                    for k in range(NB - SCALE_LATE, NB):
                        scale_block(s, k)
                if l == 2 and not first and not last:
                    for c in range(LAST_AHEAD):
                        sum_last(s, c)

            over_slabs(pool, slab)
            for k in range(NB):
                rows3(k, SLABS - 1)

        @block.vector
        def _(dve):
            linked = [0]

            def link(instruction):
                linked[0] += 1
                instruction.then_inc(dve_link, 1)
                dve.wait_ge(dve_link, linked[0])

            dve.memset(Y[:, :, D + 1:D + 2].bitcast(F32), 1.0)
            dve.memset(Y[:, :, YW - 1:YW].bitcast(F32), 0.0).then_inc(dve_link, 1)
            linked[0] += 1
            dve.sem_inc(bank_read, BANKS)
            dve.sem_inc(product, BANKS)
            for h in range(2):
                cols = slice(NB // 2 * h, NB // 2 * (h + 1))
                squares = att[:, 0, N // 2 * h:N // 2 * (h + 1)].rearrange("p (b d) -> p b d", d=D)
                dve.wait_ge(x_in[h], 16)
                link(dve.tensor_tensor(squares, x_nat[:, cols, :], x_nat[:, cols, :], ALU.mult))
                link(dve.tensor_reduce(small[:, X_SS, cols], squares, AX.X, ALU.add))
                dve.tensor_scalar(small[:, X_SS, cols], small[:, X_SS, cols], MIN_NORM ** 2, None,
                                  ALU.max).then_inc(x_ss, 1)
            for g in range(SLABS):
                dve.wait_ge(squared, g + 1)
                dve.tensor_reduce(small[:, M_SS, Q * g:Q * (g + 1)], by_block(spare(4 + g % 2)), AX.X,
                                  ALU.add).then_inc(squares_read, 1)
                if g % 4 == 3:
                    cols = slice(NB // 2 * (g // 4), NB // 2 * (g // 4 + 1))
                    dve.wait_ge(squares_read, g + 1)
                    dve.tensor_scalar(small[:, M_SS, cols], small[:, M_SS, cols], MIN_NORM ** 2, None,
                                      ALU.max).then_inc(m_ss, 1)
            dve.wait_ge(x_norms, 2)
            link(dve.tensor_scalar(small[:, G_CLIP, :], small[:, X_N, :], 1.0 - EPS, None, ALU.min))
            link(dve.tensor_scalar(small[:, G_MINUS, :], small[:, G_CLIP, :], -1.0, 1.0, ALU.mult, ALU.add))
            link(dve.reciprocal(small[:, G_H, :], small[:, G_MINUS, :]))
            dve.scalar_tensor_tensor(small[:, G_RATIO, :], small[:, G_CLIP, :], 1.0, small[:, G_H, :],
                                     ALU.add, ALU.mult).then_inc(ratio_done, 1)
            link(dve.tensor_tensor(small[:, G_Z, :], small[:, G_CLIP, :], small[:, G_CLIP, :], ALU.mult))
            link(dve.tensor_scalar(small[:, G_H, :], small[:, G_Z, :], 1.0 / 9, None, ALU.mult))
            for c in (7, 5, 3):
                link(dve.scalar_tensor_tensor(small[:, G_H, :], small[:, G_H, :], 1.0 / c, small[:, G_Z, :],
                                              ALU.add, ALU.mult))
            link(dve.scalar_tensor_tensor(small[:, G_SER, :], small[:, G_H, :], 1.0, small[:, G_CLIP, :],
                                          ALU.add, ALU.mult))
            dve.wait_ge(log_done, 1)
            link(dve.scalar_tensor_tensor(small[:, G_SER, :], small[:, G_LOG, :], -0.5, small[:, G_SER, :],
                                          ALU.mult, ALU.add))
            link(dve.scalar_tensor_tensor(small[:, G_SER, :], small[:, G_CLIP, :], TINY_ARTANH, small[:, G_SER, :],
                                          ALU.is_lt, ALU.mult))
            link(dve.scalar_tensor_tensor(small[:, G_ART, :], small[:, G_LOG, :], 0.5, small[:, G_SER, :],
                                          ALU.mult, ALU.add))
            link(dve.reciprocal(small[:, G_Z, :], small[:, X_N, :]))
            dve.wait_ge(m_norms, 2)
            link(dve.tensor_tensor(small[:, G_Z, :], small[:, G_Z, :], small[:, M_N, :], ALU.mult))
            dve.tensor_tensor(small[:, G_ART, :], small[:, G_ART, :], small[:, G_Z, :], ALU.mult).then_inc(u_done, 1)
            dve.wait_ge(tanh_done, 1)
            link(dve.tensor_scalar(small[:, G_SER, :], small[:, G_Z, :], 1.0, None, ALU.add))
            link(dve.reciprocal(small[:, G_SER, :], small[:, G_SER, :]))
            link(dve.tensor_tensor(small[:, G_SER, :], small[:, G_SER, :], small[:, G_SER, :], ALU.mult))
            link(dve.scalar_tensor_tensor(small[:, G_SER, :], small[:, G_Z, :], 4.0, small[:, G_SER, :],
                                          ALU.mult, ALU.mult))
            link(dve.tensor_scalar(small[:, G_SER, :], small[:, G_SER, :], EPS, None, ALU.max))
            link(dve.reciprocal(small[:, G_SER, :], small[:, G_SER, :]))
            link(dve.tensor_scalar(small[:, G_CLIP, :], small[:, G_SER, :], 2.0, -1.0, ALU.mult, ALU.add))
            dve.tensor_copy(Y[:, :, D], small[:, G_CLIP, :]).then_inc(dve_link, 1)
            linked[0] += 1
            link(dve.reciprocal(small[:, G_RATIO, :], small[:, M_N, :]))
            dve.tensor_tensor(Y[:, :, LO + D], small[:, G_CLIP, :], Y[:, :, D].bitcast(F32), ALU.subtract)
            link(dve.tensor_tensor(small[:, G_RATIO, :], small[:, G_RATIO, :], small[:, G_H, :], ALU.mult))
            dve.scalar_tensor_tensor(small[:, G_SER, :], small[:, G_SER, :], 2.0, small[:, G_RATIO, :],
                                     ALU.mult, ALU.mult).then_inc(y_scales, 1)
            dve.wait_ge(inputs_in, LOADS * 16)
            dve.wait_ge(exp_alpha, 1)
            link(dve.tensor_scalar(scal[:, 3:4], scal[:, 2:3], 1.0, None, ALU.add))
            link(dve.reciprocal(scal[:, 4:5], scal[:, 3:4]))
            dve.tensor_scalar(scal[:, 6:7], scal[:, 4:5], -1.0, None, ALU.mult)
            dve.tensor_scalar(scal[:, 5:6], scal[:, 1:2], 1.0 / XN_SCALE ** 2, None, ALU.mult)
            link(dve.tensor_tensor(half_bias[:], gate_bias[:, 1:3], gate_bias[:, 4:6], ALU.add))
            dve.tensor_scalar(half_bias[:], half_bias[:], 0.5, None, ALU.mult)

            def read_bank(l, s, k, first):
                kind, j = fill_list(l, s)[k]
                b = strip[k % BANKS]
                if kind == "S":
                    c, q = j // Q, j % Q
                    if q == 0:
                        wait_apart(dve, tile_in[c], (s + (SLABS * l + 1)) * 16)
                    if first and q == Q - 1:
                        dve.wait_ge(y_ready, SLABS * 2 + c + 1)
                    wait_apart(dve, filled, fills(l, s, k))
                    dve.tensor_tensor_reduce(att[:, q, SLAB * c:SLAB * (c + 1)], b[:], tile[:, c, q, :],
                                             scal[:, 5:6], NEG_HUGE, ALU.mult, ALU.max,
                                             peak[:, c, q:q + 1]).then_inc(bank_read, 1)
                    if q == Q - 1 or c == SLABS - 1:
                        of = slice(q, q + 1) if c == SLABS - 1 else slice(0, Q)
                        dve.wait_ge(bank_read, fills(l, s, k) + BANKS)
                        dve.tensor_scalar(neg_peak[:, c, of], peak[:, c, of], -1.0, None, ALU.mult).then_inc(peaks, 1)
                    return
                n = nth_strip(l, s, k) % BANKS
                dve.wait_ge(hi_done, strips_done(l, s, k))
                dve.tensor_tensor(part_l[:, n, :], b[:], part_h[:, n, :].bitcast(F32),
                                  ALU.subtract).then_inc(bank_read, 1)
                if kind == "C" and j + WEIGHED_AHEAD < NB:
                    weigh_block(s - 1, j + WEIGHED_AHEAD)

            def weigh_block(s, i):
                c, q = i // Q, i % Q
                if q == Q - 1 and not (isinstance(s, int) and s == 0):
                    return
                mine = att[:, q, SLAB * c:SLAB * (c + 1)]
                dve.wait_ge(adj_scaled, s * NB + (i + 1))
                block_done = dve.scalar_tensor_tensor(mine, mine, weight[:, c, q:q + 1], tile[:, c, q, :],
                                                      ALU.mult, ALU.add)
                if q >= Q - 2:
                    block_done.then_inc(weighed if q == Q - 2 else last_weighed, 1)

            def weigh_rows(s):
                def before(name):
                    dve.wait_ge(weigh, weigh_before(s, name))
                row_peak, row_sum, inverse = [row_value[:, i, :] for i in range(3)]
                if not isinstance(s, int) or s > 0:
                    before("peak")
                dve.tensor_reduce(row_peak, peak[:].rearrange("p c q -> p q c"), AX.X, ALU.max).then_inc(weigh, 1)
                before("gap")
                dve.tensor_tensor(shrink[:], peak[:], row_peak.unsqueeze(1).to_broadcast([P, SLABS, Q]),
                                  ALU.subtract).then_inc(weigh, 1)
                dve.wait_ge(exps, s * SLABS + SLABS)
                before("shrunk_sums")
                dve.tensor_tensor(exp_sum[:], exp_sum[:], shrink[:], ALU.mult).then_inc(weigh, 1)
                before("row_sums")
                dve.tensor_reduce(row_sum, exp_sum[:].rearrange("p c q -> p q c"), AX.X, ALU.add).then_inc(weigh, 1)
                dve.wait_ge(own_dis_in, s + 1)
                before("times_dis")
                dve.tensor_tensor(row_sum, row_sum, own_dis[:], ALU.mult).then_inc(weigh, 1)
                before("inverse")
                dve.reciprocal(inverse, row_sum).then_inc(weigh, 1)
                before("weights")
                dve.scalar_tensor_tensor(weight[:], shrink[:], scal[:, 4:5],
                                         inverse.unsqueeze(1).to_broadcast([P, SLABS, Q]), ALU.mult,
                                         ALU.mult).then_inc(weigh, 1)
                dve.wait_ge(weigh, s * len(WEIGH) + len(WEIGH))
                for i in range(WEIGHED_AHEAD):
                    weigh_block(s, i)

            def read_acc(s):
                dve.wait_ge(product, slab_done(0, s) + BANKS)
                dve.tensor_copy(nat[:, 2, :], acc0[2][:, 0:YW])
                dve.tensor_copy(nat[:, 3, :], acc0[3][:, 0:YW]).then_inc(acc_read, 1)

            def layer_norm(l, k, s, to):
                def before(name):
                    dve.wait_ge(row, row_before(l, s, name))

                def before_apart(name):
                    wait_apart(dve, row, row_before(l, s, name))
                if k == 0:
                    before("ln_stats")
                    for q in range(Q):
                        last = dve.bn_stats(stats[:, q, :], t[:, q, :])
                    last.then_inc(row, 1)
                if k == 1:
                    before_apart("ln_aggr")
                    for q in range(Q):
                        last = dve.bn_aggr(mv[:, q, :], stats[:, q, :])
                    last.then_inc(row, 1)
                    before("ln_eps")
                    dve.tensor_scalar(sc[:, VAR, :], mv[:, :, 1], EPS, None, ALU.add).then_inc(row, 1)
                if k == 2:
                    before("ln_bias")
                    dve.scalar_tensor_tensor(sc[:, BIAS, :], mv[:, :, 0], -1.0, sc[:, RSTD, :], ALU.mult,
                                             ALU.mult).then_inc(row, 1)
                    before("ln_out")
                if k in (2, 3):
                    for q in (0, 1) if k == 2 else (2, 3):
                        last = dve.tensor_scalar(to(q), t[:, q, :], sc[:, RSTD, q:q + 1], sc[:, BIAS, q:q + 1],
                                                 ALU.mult, ALU.add)
                if k == 3:
                    last.then_inc(row, 1)

            def rows0(k, s):
                def before(name):
                    dve.wait_ge(row, row_before(0, s, name))

                def before_apart(name):
                    wait_apart(dve, row, row_before(0, s, name))

                def val(i):
                    return sc[:, i, :]
                total = nat[:, :, D + 1]
                if k == 5:
                    before("degrees")
                    dve.tensor_scalar(val(Z), total, 1.0, 0.0, ALU.add, ALU.is_equal)
                    dve.tensor_scalar(val(KEEP), total, 1.0, 0.0, ALU.add, ALU.not_equal)
                    dve.tensor_scalar(val(ZERO), total, 1.0, None, ALU.max)
                    dve.scalar_tensor_tensor(val(ABS), val(DEN), -1.0, val(DEN), ALU.mult, ALU.max)
                    dve.tensor_scalar(val(SIGN), val(DEN), 0.0, 2.0, ALU.is_ge, ALU.mult).then_inc(row, 1)
                if k == 6:
                    before("abs_floor")
                    dve.tensor_scalar(val(ABS), val(ABS), DEN_EPS, None, ALU.max).then_inc(row, 1)
                    before("inv_abs")
                    dve.scalar_tensor_tensor(val(SAFE), total, 1.0, val(Z), ALU.add, ALU.add)
                    dve.reciprocal(val(INV_ABS), val(ABS)).then_inc(row, 1)
                    before("inv_den")
                    dve.scalar_tensor_tensor(val(INV), val(SIGN), -1.0, val(INV_ABS), ALU.add,
                                             ALU.mult).then_inc(row, 1)
                if k == 8:
                    before("norm_den")
                    dve.tensor_tensor(val(NRM), val(NRM), val(INV_ABS), ALU.mult).then_inc(row, 1)
                    before("floor_clip")
                    dve.tensor_scalar(val(CLIP), val(NRM), MIN_NORM, 1.0 - EPS, ALU.max, ALU.min)
                    dve.tensor_scalar(val(UNIT), val(NRM), MIN_NORM, None, ALU.max).then_inc(row, 1)
                if k == 9:
                    before("artanh_a")
                    dve.tensor_scalar(val(MINUS), val(CLIP), -1.0, 1.0, ALU.mult, ALU.add)
                    dve.tensor_tensor(val(Z), val(CLIP), val(CLIP), ALU.mult)
                    dve.scalar_tensor_tensor(val(H), val(CLIP), 1.0 / 9, val(CLIP), ALU.mult, ALU.mult)
                    dve.reciprocal(val(INV_NRM), val(UNIT)).then_inc(row, 1)
                    before("artanh_b")
                    dve.reciprocal(val(RATIO), val(MINUS))
                    dve.scalar_tensor_tensor(val(SER), val(H), 1.0 / 7, val(Z), ALU.add, ALU.mult)
                    dve.tensor_tensor(val(UNIT), val(INV), val(INV_NRM), ALU.mult).then_inc(row, 1)
                if k == 10:
                    before("ratio")
                    dve.scalar_tensor_tensor(val(H), val(SER), 1.0 / 5, val(Z), ALU.add, ALU.mult)
                    dve.scalar_tensor_tensor(val(RATIO), val(CLIP), 1.0, val(RATIO), ALU.add,
                                             ALU.mult).then_inc(row, 1)
                    before("h4")
                    dve.scalar_tensor_tensor(val(H), val(H), 1.0 / 3, val(Z), ALU.add, ALU.mult).then_inc(row, 1)
                if k == 12:
                    before("series")
                    dve.scalar_tensor_tensor(val(SER), val(H), 1.0, val(CLIP), ALU.add, ALU.mult).then_inc(row, 1)
                if k == 13:
                    before("differ")
                    dve.scalar_tensor_tensor(val(SER), val(LOG), -0.5, val(SER), ALU.mult, ALU.add).then_inc(row, 1)
                    before("choose")
                    dve.scalar_tensor_tensor(val(SER), val(CLIP), TINY_ARTANH, val(SER), ALU.is_lt,
                                             ALU.mult).then_inc(row, 1)
                if k == 14:
                    before("artanh")
                    dve.scalar_tensor_tensor(val(ART), val(LOG), 0.5, val(SER), ALU.mult, ALU.add).then_inc(row, 1)
                    before("scale")
                    dve.scalar_tensor_tensor(val(SCL), val(ART), 0.5, total, ALU.mult, ALU.mult).then_inc(row, 1)
                if k == 15:
                    before("scale_clip")
                    dve.tensor_scalar(val(SCL), val(SCL), ARTANH_MAX, -ARTANH_MAX, ALU.min, ALU.max).then_inc(row, 1)
                    before("scale_row")
                    dve.tensor_tensor(val(SCL), val(SCL), val(UNIT), ALU.mult).then_inc(row, 1)
                if k == 18:
                    before("clamp_u")
                    dve.tensor_scalar(val(SS), val(SS), MIN_NORM ** 2, None, ALU.max).then_inc(row, 1)
                if k == 20:
                    before("inv_u")
                    dve.reciprocal(val(INV), val(NRM)).then_inc(row, 1)
                    before("scale_u")
                    dve.tensor_tensor(val(SCL), val(H), val(INV), ALU.mult).then_inc(row, 1)
                if k in (22, 23, 25, 26):
                    layer_norm(0, (22, 23, 25, 26).index(k), s, lambda q: x_nat[:, bass.ds(s * Q + q, 1), :])

            def rows1(k, s):
                def before(name):
                    dve.wait_ge(row, row_before(1, s, name))

                def before_apart(name):
                    wait_apart(dve, row, row_before(1, s, name))
                if k in (7, 8):
                    if k == 7:
                        before("combine")
                    for q in (0, 1) if k == 7 else (2, 3):
                        last = dve.scalar_tensor_tensor(t[:, q, :], rows_a[:, P * q:P * (q + 1)],
                                                        d_rows[:, q:q + 1], v[:, q, :], ALU.mult, ALU.add)
                    if k == 8:
                        last.then_inc(row, 1)
                if k in (10, 11, 13, 14):
                    layer_norm(1, (10, 11, 13, 14).index(k), s, lambda q: x_nat[:, bass.ds(s * Q + q, 1), :])
                if k == 17:
                    before("sum_x")
                    dve.tensor_reduce(sc[:, SS, :], v[:], AX.X, ALU.add).then_inc(row, 1)
                if k == 18:
                    before("clamp_x")
                    dve.tensor_scalar(sc[:, SS, :], sc[:, SS, :], COS_EPS ** 2, None, ALU.max).then_inc(row, 1)
                if k in (21, 22):
                    if k == 21:
                        before("unit")
                    for q in (0, 1) if k == 21 else (2, 3):
                        last = dve.tensor_scalar(v[:, q, :], x_nat[:, bass.ds(s * Q + q, 1), :], sc[:, H, q:q + 1],
                                                 XN_SCALE, ALU.mult, ALU.mult)
                    if k == 22:
                        last.then_inc(row, 1)
                if k == 27:
                    before("unit_low")
                    mine = bass.ds(s * SLAB, SLAB)
                    dve.tensor_tensor(unit_l[:, mine], rows_b[:], unit_h[:, mine], ALU.subtract).then_inc(row, 1)

            def rows2(k, s):
                def before(name):
                    dve.wait_ge(row, row_before(2, s, name))

                def before_apart(name):
                    wait_apart(dve, row, row_before(2, s, name))
                if k == 11:
                    before("x_scale")
                    dve.tensor_scalar(v[:], v[:], scal[:, 6:7], None, ALU.mult).then_inc(row, 1)
                if k in (12, 14):
                    if k == 12:
                        before("combine")
                    for q in (0, 1) if k == 12 else (2, 3):
                        last = dve.scalar_tensor_tensor(t[:, q, :], rows_a[:, P * q:P * (q + 1)],
                                                        sc[:, DEN, q:q + 1], v[:, q, :], ALU.mult, ALU.add)
                    if k == 14:
                        last.then_inc(row, 1)
                if k in (18, 19, 21, 22):
                    layer_norm(2, (18, 19, 21, 22).index(k), s, lambda q: v[:, q, :])

            def rows3(k, s):
                def before(name):
                    dve.wait_ge(row, row_before(3, s, name))

                def before_apart(name):
                    wait_apart(dve, row, row_before(3, s, name))
                if k == 18:
                    before("r_times")
                    dve.scalar_tensor_tensor(spare(2), rows_a[:], gate_bias[:, 6:7], spare(2), ALU.add,
                                             ALU.mult).then_inc(row, 1)
                if k == 19:
                    before("n_in")
                    dve.tensor_tensor(spare(2), rows_b[:], spare(2), ALU.add).then_inc(row, 1)
                if k == 26:
                    before("combine")
                    dve.tensor_tensor(t[:].rearrange("p q d -> p (q d)"), rows_a[:],
                                      t[:].rearrange("p q d -> p (q d)"), ALU.add).then_inc(row, 1)
                if k in (27, 28, 29, 30):
                    if k == 29:
                        dve.wait_ge(kept, s * 16 + 16 * SLABS)
                    layer_norm(3, (27, 28, 29, 30).index(k), s, lambda q: v[:, q, :])

            rows = [rows0, rows1, rows2, rows3]

            def slab(l, s, first=False, last=False):
                lp, sp_ = previous(l, s, first)
                for k in range(len(fill_list(l, s))):
                    if k == AHEAD and lp == 0:
                        read_acc(sp_)
                    read_bank(l, s, k, first)
                    if lp >= 0:
                        rows[lp](k, sp_)
                if l == 2 and not last:
                    weigh_rows(s)

            over_slabs(dve, slab)
            for k in range(NB):
                rows3(k, SLABS - 1)


_INS = ["x", "adj", "L0_gnn_W", "L1_gnn_W", "L1_gnn_b", "L2_gnn_alpha", "L2_gnn_beta", "L3_gnn_W_msg",
        "L3_gnn_b_msg", "L3_gnn_W_ih", "L3_gnn_W_hh", "L3_gnn_b_ih", "L3_gnn_b_hh"]


def kernel(**inputs):
    import concourse.bacc as bacc
    from concourse.bass_utils import run_bass_kernel_spmd

    nc = bacc.Bacc("TRN2", target_bir_lowering=False, num_devices=1)
    arrays, aps = {}, []
    for name in _INS:
        a = np.ascontiguousarray(inputs[name])
        a = a.reshape(1) if a.ndim == 0 else a
        arrays[f"in_{name}"] = a
        aps.append(nc.dram_tensor(f"in_{name}", a.shape, mybir.dt.from_np(a.dtype), kind="ExternalInput").ap())
    out = nc.dram_tensor("out", (N, D), F32, kind="ExternalOutput").ap()
    scratch = nc.dram_tensor("scratch", (N, D), F32, kind="Internal").ap()
    dis_out = nc.dram_tensor("dis_out", (N,), F32, kind="Internal").ap()
    build(nc, *aps, out, scratch, dis_out)
    got = run_bass_kernel_spmd(nc, [arrays], core_ids=[0])
    return got.results[0]["out"]
```
